# Optimizing a Trainium2 kernel written in Bass

```python
import numpy as np
import jax
import jax.numpy as jnp

def _softmax(x, axis=-1):
    return jax.nn.softmax(x, axis=axis)

def _gelu(x):
    return jax.nn.gelu(x, approximate=True)

def _silu(x):
    return jax.nn.silu(x)

def _sigmoid(x):
    return jax.nn.sigmoid(x)

def _layernorm(x, axis=-1, eps=1e-05):
    m = jnp.mean(x, axis=axis, keepdims=True)
    v = jnp.var(x, axis=axis, keepdims=True)
    return (x - m) / jnp.sqrt(v + eps)

def _scatter_add(tgt, idx, src, axis=0):
    return tgt.at[idx].add(src)

def _segment_sum(src, seg, n):
    return jax.ops.segment_sum(src, seg, n)
kernel_name = 'mk_xattn_ffn_d2_seqx_r4_28ab5e'

def setup_inputs(seed: int=0):
    np.random.seed(seed)
    _w = jnp.asarray

    def _rec_inputs():
        import jax
        import jax.numpy as jnp
        _rk = jax.random.key(seed)
        x = -0.0002928 + 1 * jax.random.normal(jax.random.fold_in(_rk, 1), (4, 512, 256), jnp.float32)
        _lenS = 512 - jax.random.randint(jax.random.fold_in(_rk, 7), (4,), 0, max(1, 512 // 4) + 1, jnp.int32)
        _lenS2 = 512 - jax.random.randint(jax.random.fold_in(_rk, 8), (4,), 0, max(1, 512 // 4) + 1, jnp.int32)
        _ctx_1024P = jax.random.normal(jax.random.fold_in(_rk, 11), (4, 16, 256), jnp.float32)
        _ctx_1024c = jax.random.dirichlet(jax.random.fold_in(_rk, 511), 0.3 * jnp.ones((16,), jnp.float32), (4, 512))
        _ctx_1024t = jnp.einsum('bsk,bkd->bsd', _ctx_1024c, _ctx_1024P)
        _ctx_1024t = _ctx_1024t * jax.lax.rsqrt(jnp.mean(jnp.square(_ctx_1024t)) + 1e-12) * 0.953939
        ctx_1024 = -1.39393e-06 + 0.999914 * (_ctx_1024t + 0.3 * jax.random.normal(jax.random.fold_in(_rk, 611), (4, 512, 256), jnp.float32))
        return (x, ctx_1024)
    x, ctx_1024 = _rec_inputs()

    def _L0_xattn_setup():
        import jax, jax.numpy as jnp
        import numpy as np
        import math
        D_MODEL = 256
        NUM_HEADS = 16
        MAX_LEN = 512
        D_HEAD = D_MODEL // NUM_HEADS
        BATCH = 2
        SEQ = 512

        def _skew(QEr):
            B, H, R, C = QEr.shape
            padded = jnp.pad(QEr, ((0, 0), (0, 0), (0, 0), (1, 0)))
            reshaped = padded.reshape(B, H, C + 1, R)
            return reshaped[:, :, 1:, :]
        root = jax.random.key(seed)
        ks = jax.random.split(root, 10)
        s = 1.0 / math.sqrt(D_MODEL)
        return {'query': jax.random.normal(ks[0], (BATCH, SEQ, D_MODEL), jnp.float32), 'key': jax.random.normal(ks[1], (BATCH, SEQ, D_MODEL), jnp.float32), 'value': jax.random.normal(ks[2], (BATCH, SEQ, D_MODEL), jnp.float32), 'Wq': jax.random.normal(ks[3], (D_MODEL, D_MODEL), jnp.float32) * s, 'bq': jax.random.normal(ks[4], (D_MODEL,), jnp.float32) * s, 'Wk': jax.random.normal(ks[5], (D_MODEL, D_MODEL), jnp.float32) * s, 'bk': jax.random.normal(ks[6], (D_MODEL,), jnp.float32) * s, 'Wv': jax.random.normal(ks[7], (D_MODEL, D_MODEL), jnp.float32) * s, 'bv': jax.random.normal(ks[8], (D_MODEL,), jnp.float32) * s, 'Er': jax.random.normal(ks[9], (MAX_LEN, D_HEAD), jnp.float32)}
    _L0_xattn_all = _L0_xattn_setup()
    _L0_xattn_in = {k: v for k, v in _L0_xattn_all.items() if k in ('Wq', 'bq', 'Wk', 'bk', 'Wv', 'bv', 'Er')}
    del _L0_xattn_all

    def _L0_ffn_setup():
        import jax, jax.numpy as jnp
        import numpy as np
        D_MODEL = 256
        N_HEADS = 16
        HEAD_DIM = D_MODEL // N_HEADS
        FFN_DIM = 1024
        N_EXPERTS = 8
        TOP_K = 2
        BATCH = 4
        SEQ = 256

        def _layernorm(x, w, b, eps=1e-05):
            mu = jnp.mean(x, axis=-1, keepdims=True)
            var = jnp.mean(jnp.square(x - mu), axis=-1, keepdims=True)
            return (x - mu) * jax.lax.rsqrt(var + eps) * w + b

        def _causal_attention(nx, Wqkv, bqkv, Wo, bo):
            B, S, D = nx.shape
            qkv = nx @ Wqkv + bqkv
            q, k, v = jnp.split(qkv, 3, axis=-1)
            q = q.reshape(B, S, N_HEADS, HEAD_DIM)
            k = k.reshape(B, S, N_HEADS, HEAD_DIM)
            v = v.reshape(B, S, N_HEADS, HEAD_DIM)
            scores = jnp.einsum('bqhd,bkhd->bhqk', q, k) / jnp.sqrt(jnp.float32(HEAD_DIM))
            causal = jnp.tril(jnp.ones((S, S), bool))
            scores = jnp.where(causal, scores, jnp.finfo(scores.dtype).min)
            attn = jax.nn.softmax(scores, axis=-1)
            out = jnp.einsum('bhqk,bkhd->bqhd', attn, v).reshape(B, S, D)
            return out @ Wo + bo

        def _moe_ffn(nx, gate_W, fc1_w, fc1_b, fc2_w, fc2_b):
            gate_logits = nx @ gate_W
            topk_vals, topk_idx = jax.lax.top_k(gate_logits, TOP_K)
            gate_w = jax.nn.softmax(topk_vals, axis=-1)
            dense_gates = jnp.sum(jax.nn.one_hot(topk_idx, N_EXPERTS, dtype=nx.dtype) * gate_w[..., None], axis=-2)
            moe_out = jnp.zeros_like(nx)
            for e in range(N_EXPERTS):
                h = jax.nn.gelu(jnp.einsum('bsd,fd->bsf', nx, fc1_w[e]) + fc1_b[e], approximate=False)
                y = jnp.einsum('bsf,df->bsd', h, fc2_w[e]) + fc2_b[e]
                moe_out = moe_out + y * dense_gates[..., e:e + 1]
            return moe_out
        key = jax.random.key(seed)
        ks = jax.random.split(key, 12)
        s = lambda k, shape, scale: jax.random.normal(k, shape, dtype=jnp.float32) * scale
        inp = {'x': s(ks[0], (BATCH, SEQ, D_MODEL), 1.0), 'ln1_w': jnp.ones((D_MODEL,), jnp.float32), 'ln1_b': jnp.zeros((D_MODEL,), jnp.float32), 'ln2_w': jnp.ones((D_MODEL,), jnp.float32), 'ln2_b': jnp.zeros((D_MODEL,), jnp.float32), 'Wqkv': s(ks[1], (D_MODEL, 3 * D_MODEL), 0.02), 'bqkv': jnp.zeros((3 * D_MODEL,), jnp.float32), 'Wo': s(ks[2], (D_MODEL, D_MODEL), 0.02), 'bo': jnp.zeros((D_MODEL,), jnp.float32), 'gate_W': s(ks[3], (D_MODEL, N_EXPERTS), 0.02), 'fc1_w': s(ks[4], (N_EXPERTS, FFN_DIM, D_MODEL), (2.0 / D_MODEL) ** 0.5), 'fc1_b': jnp.zeros((N_EXPERTS, FFN_DIM), jnp.float32), 'fc2_w': s(ks[5], (N_EXPERTS, D_MODEL, FFN_DIM), (1.0 / FFN_DIM) ** 0.5), 'fc2_b': jnp.zeros((N_EXPERTS, D_MODEL), jnp.float32)}
        return inp
    _L0_ffn_all = _L0_ffn_setup()
    _L0_ffn_in = {k: v for k, v in _L0_ffn_all.items() if k in ('ln1_w', 'ln1_b', 'ln2_w', 'ln2_b', 'Wqkv', 'bqkv', 'Wo', 'bo', 'gate_W', 'fc1_w', 'fc1_b', 'fc2_w', 'fc2_b')}
    del _L0_ffn_all

    def _L1_xattn_setup():
        import jax, jax.numpy as jnp
        import numpy as np
        B, S, D = (4, 512, 256)
        H, HD = (16, 64)
        key = jax.random.key(seed)
        ks = jax.random.split(key, 11)
        s = 0.02
        return {'inputs_q': jax.random.normal(ks[0], (B, S, D), jnp.float32), 'inputs_k': jax.random.normal(ks[1], (B, S, D), jnp.float32), 'inputs_v': jax.random.normal(ks[2], (B, S, D), jnp.float32), 'Wq': jax.random.normal(ks[3], (D, H, HD), jnp.float32) * s, 'bq': jnp.zeros((H, HD), jnp.float32), 'Wk': jax.random.normal(ks[4], (D, H, HD), jnp.float32) * s, 'bk': jnp.zeros((H, HD), jnp.float32), 'Wv': jax.random.normal(ks[5], (D, H, HD), jnp.float32) * s, 'bv': jnp.zeros((H, HD), jnp.float32), 'Wo': jax.random.normal(ks[6], (H, HD, D), jnp.float32) * s, 'bo': jnp.zeros((D,), jnp.float32)}
    _L1_xattn_all = _L1_xattn_setup()
    _L1_xattn_in = {k: v for k, v in _L1_xattn_all.items() if k in ('Wq', 'bq', 'Wk', 'bk', 'Wv', 'bv', 'Wo', 'bo')}
    del _L1_xattn_all

    def _L1_ffn_setup():
        import jax, jax.numpy as jnp
        import numpy as np
        HIDDEN = 256
        NUM_EXPERTS = 16
        TOP_K = 6
        EPS = 1e-10
        key = jax.random.key(seed)
        k1, k2, k3, k4 = jax.random.split(key, 4)
        tokens = jax.random.normal(k1, (4, 512, HIDDEN), dtype=jnp.float32)
        bound = 1.0 / np.sqrt(HIDDEN)
        router_w = jax.random.uniform(k2, (NUM_EXPERTS, HIDDEN), jnp.float32, -bound, bound)
        router_b = jax.random.uniform(k3, (NUM_EXPERTS,), jnp.float32, -bound, bound)
        expert_w = jax.random.normal(k4, (NUM_EXPERTS, HIDDEN, HIDDEN), dtype=jnp.float32) / np.sqrt(HIDDEN)
        return {'tokens': tokens, 'router_w': router_w, 'router_b': router_b, 'expert_w': expert_w}
    _L1_ffn_all = _L1_ffn_setup()
    _L1_ffn_in = {k: v for k, v in _L1_ffn_all.items() if k in ('router_w', 'router_b', 'expert_w')}
    del _L1_ffn_all
    return {'x': x, 'ctx_1024': ctx_1024, 'L0_xattn_Wq': _L0_xattn_in['Wq'], 'L0_xattn_bq': _L0_xattn_in['bq'], 'L0_xattn_Wk': _L0_xattn_in['Wk'], 'L0_xattn_bk': _L0_xattn_in['bk'], 'L0_xattn_Wv': _L0_xattn_in['Wv'], 'L0_xattn_bv': _L0_xattn_in['bv'], 'L0_xattn_Er': _L0_xattn_in['Er'], 'L0_ffn_ln1_w': _L0_ffn_in['ln1_w'], 'L0_ffn_ln1_b': _L0_ffn_in['ln1_b'], 'L0_ffn_ln2_w': _L0_ffn_in['ln2_w'], 'L0_ffn_ln2_b': _L0_ffn_in['ln2_b'], 'L0_ffn_Wqkv': _L0_ffn_in['Wqkv'], 'L0_ffn_bqkv': _L0_ffn_in['bqkv'], 'L0_ffn_Wo': _L0_ffn_in['Wo'], 'L0_ffn_bo': _L0_ffn_in['bo'], 'L0_ffn_gate_W': _L0_ffn_in['gate_W'], 'L0_ffn_fc1_w': _L0_ffn_in['fc1_w'], 'L0_ffn_fc1_b': _L0_ffn_in['fc1_b'], 'L0_ffn_fc2_w': _L0_ffn_in['fc2_w'], 'L0_ffn_fc2_b': _L0_ffn_in['fc2_b'], 'L1_xattn_Wq': _L1_xattn_in['Wq'], 'L1_xattn_bq': _L1_xattn_in['bq'], 'L1_xattn_Wk': _L1_xattn_in['Wk'], 'L1_xattn_bk': _L1_xattn_in['bk'], 'L1_xattn_Wv': _L1_xattn_in['Wv'], 'L1_xattn_bv': _L1_xattn_in['bv'], 'L1_xattn_Wo': _L1_xattn_in['Wo'], 'L1_xattn_bo': _L1_xattn_in['bo'], 'L1_ffn_router_w': _L1_ffn_in['router_w'], 'L1_ffn_router_b': _L1_ffn_in['router_b'], 'L1_ffn_expert_w': _L1_ffn_in['expert_w']}

def reference(x, ctx_1024, L0_xattn_Wq, L0_xattn_bq, L0_xattn_Wk, L0_xattn_bk, L0_xattn_Wv, L0_xattn_bv, L0_xattn_Er, L0_ffn_ln1_w, L0_ffn_ln1_b, L0_ffn_ln2_w, L0_ffn_ln2_b, L0_ffn_Wqkv, L0_ffn_bqkv, L0_ffn_Wo, L0_ffn_bo, L0_ffn_gate_W, L0_ffn_fc1_w, L0_ffn_fc1_b, L0_ffn_fc2_w, L0_ffn_fc2_b, L1_xattn_Wq, L1_xattn_bq, L1_xattn_Wk, L1_xattn_bk, L1_xattn_Wv, L1_xattn_bv, L1_xattn_Wo, L1_xattn_bo, L1_ffn_router_w, L1_ffn_router_b, L1_ffn_expert_w):
    import jax
    import jax.numpy as jnp

    def _L0_xattn_ref(query, key, value, Wq, bq, Wk, bk, Wv, bv, Er):
        import jax, jax.numpy as jnp
        import numpy as np
        import math
        D_MODEL = 256
        NUM_HEADS = 16
        MAX_LEN = 512
        D_HEAD = D_MODEL // NUM_HEADS
        BATCH = 2
        SEQ = 512

        def _skew(QEr):
            B, H, R, C = QEr.shape
            padded = jnp.pad(QEr, ((0, 0), (0, 0), (0, 0), (1, 0)))
            reshaped = padded.reshape(B, H, C + 1, R)
            return reshaped[:, :, 1:, :]
        B, S, D = query.shape
        H, dh = (NUM_HEADS, D_HEAD)
        q = (jnp.einsum('bsd,ed->bse', query, Wq) + bq).reshape(B, S, H, dh).transpose(0, 2, 1, 3)
        k = (jnp.einsum('bsd,ed->bse', key, Wk) + bk).reshape(B, S, H, dh).transpose(0, 2, 1, 3)
        v = (jnp.einsum('bsd,ed->bse', value, Wv) + bv).reshape(B, S, H, dh).transpose(0, 2, 1, 3)
        start = MAX_LEN - S
        Er_s = Er[start:, :]
        QEr = jnp.einsum('bhsd,ld->bhsl', q, Er_s)
        Srel = _skew(QEr)
        QK = jnp.einsum('bhsd,bhtd->bhst', q, k)
        attn = (QK + Srel) / math.sqrt(dh)
        causal = jnp.tril(jnp.ones((S, S), dtype=bool))
        attn = jnp.where(causal[None, None], attn, -jnp.inf)
        attn = jax.nn.softmax(attn, axis=-1)
        out = jnp.einsum('bhst,bhtd->bhsd', attn, v)
        out = out.transpose(0, 2, 1, 3).reshape(B, S, D)
        return out

    def _L0_ffn_ref(x, ln1_w, ln1_b, ln2_w, ln2_b, Wqkv, bqkv, Wo, bo, gate_W, fc1_w, fc1_b, fc2_w, fc2_b):
        import jax, jax.numpy as jnp
        import numpy as np
        D_MODEL = 256
        N_HEADS = 16
        HEAD_DIM = D_MODEL // N_HEADS
        FFN_DIM = 1024
        N_EXPERTS = 8
        TOP_K = 2
        BATCH = 4
        SEQ = 256

        def _layernorm(x, w, b, eps=1e-05):
            mu = jnp.mean(x, axis=-1, keepdims=True)
            var = jnp.mean(jnp.square(x - mu), axis=-1, keepdims=True)
            return (x - mu) * jax.lax.rsqrt(var + eps) * w + b

        def _causal_attention(nx, Wqkv, bqkv, Wo, bo):
            B, S, D = nx.shape
            qkv = nx @ Wqkv + bqkv
            q, k, v = jnp.split(qkv, 3, axis=-1)
            q = q.reshape(B, S, N_HEADS, HEAD_DIM)
            k = k.reshape(B, S, N_HEADS, HEAD_DIM)
            v = v.reshape(B, S, N_HEADS, HEAD_DIM)
            scores = jnp.einsum('bqhd,bkhd->bhqk', q, k) / jnp.sqrt(jnp.float32(HEAD_DIM))
            causal = jnp.tril(jnp.ones((S, S), bool))
            scores = jnp.where(causal, scores, jnp.finfo(scores.dtype).min)
            attn = jax.nn.softmax(scores, axis=-1)
            out = jnp.einsum('bhqk,bkhd->bqhd', attn, v).reshape(B, S, D)
            return out @ Wo + bo

        def _moe_ffn(nx, gate_W, fc1_w, fc1_b, fc2_w, fc2_b):
            gate_logits = nx @ gate_W
            topk_vals, topk_idx = jax.lax.top_k(gate_logits, TOP_K)
            gate_w = jax.nn.softmax(topk_vals, axis=-1)
            dense_gates = jnp.sum(jax.nn.one_hot(topk_idx, N_EXPERTS, dtype=nx.dtype) * gate_w[..., None], axis=-2)
            moe_out = jnp.zeros_like(nx)
            for e in range(N_EXPERTS):
                h = jax.nn.gelu(jnp.einsum('bsd,fd->bsf', nx, fc1_w[e]) + fc1_b[e], approximate=False)
                y = jnp.einsum('bsf,df->bsd', h, fc2_w[e]) + fc2_b[e]
                moe_out = moe_out + y * dense_gates[..., e:e + 1]
            return moe_out
        nx = _layernorm(x, ln1_w, ln1_b)
        attn_out = _causal_attention(nx, Wqkv, bqkv, Wo, bo)
        x = x + attn_out
        nx2 = _layernorm(x, ln2_w, ln2_b)
        moe_out = _moe_ffn(nx2, gate_W, fc1_w, fc1_b, fc2_w, fc2_b)
        return x + moe_out

    def _L1_xattn_ref(inputs_q, inputs_k, inputs_v, Wq, bq, Wk, bk, Wv, bv, Wo, bo):
        import jax, jax.numpy as jnp
        import numpy as np
        B, S, D = (4, 512, 256)
        H, HD = (16, 64)
        q = jnp.einsum('bsf,fhd->bshd', inputs_q, Wq) + bq
        k = jnp.einsum('bsf,fhd->bshd', inputs_k, Wk) + bk
        v = jnp.einsum('bsf,fhd->bshd', inputs_v, Wv) + bv
        depth = q.shape[-1]
        q = q / jnp.sqrt(jnp.asarray(depth, q.dtype))
        attn = jnp.einsum('bqhd,bkhd->bhqk', q, k)
        attn = jax.nn.softmax(attn, axis=-1)
        x = jnp.einsum('bhqk,bkhd->bqhd', attn, v)
        out = jnp.einsum('bqhd,hdo->bqo', x, Wo) + bo
        return out

    def _L1_ffn_ref(tokens, router_w, router_b, expert_w):
        import jax, jax.numpy as jnp
        import numpy as np
        HIDDEN = 256
        NUM_EXPERTS = 16
        TOP_K = 6
        EPS = 1e-10
        B, S, H = tokens.shape
        E = expert_w.shape[0]
        T = B * S
        logits = jnp.einsum('bsh,eh->bse', tokens, router_w) + router_b
        probs = jax.nn.softmax(logits, axis=-1)
        top_p, top_i = jax.lax.top_k(probs, TOP_K)
        top_p = top_p / (jnp.sum(top_p, axis=-1, keepdims=True) + EPS)
        x = tokens.reshape(T, H)
        flat_i = top_i.reshape(T, TOP_K)
        flat_p = top_p.reshape(T, TOP_K)
        gate = jnp.zeros((T, E), dtype=flat_p.dtype)
        gate = gate.at[jnp.arange(T)[:, None], flat_i].add(flat_p)
        acc = jnp.maximum(jnp.sum(gate, axis=-1), EPS)
        out = jnp.zeros_like(x)
        for e in range(E):
            out = out + x @ expert_w[e] * gate[:, e:e + 1]
        out = (out / acc[:, None]).reshape(B, S, H)
        out = out + EPS * jnp.sum(top_p, axis=-1, keepdims=True)
        return out
    x = x + _L0_xattn_ref(_layernorm(x, axis=-1), ctx_1024, ctx_1024, L0_xattn_Wq, L0_xattn_bq, L0_xattn_Wk, L0_xattn_bk, L0_xattn_Wv, L0_xattn_bv, L0_xattn_Er)
    x = x + _L0_ffn_ref(_layernorm(x, axis=-1), L0_ffn_ln1_w, L0_ffn_ln1_b, L0_ffn_ln2_w, L0_ffn_ln2_b, L0_ffn_Wqkv, L0_ffn_bqkv, L0_ffn_Wo, L0_ffn_bo, L0_ffn_gate_W, L0_ffn_fc1_w, L0_ffn_fc1_b, L0_ffn_fc2_w, L0_ffn_fc2_b)
    x = x + _L1_xattn_ref(_layernorm(x, axis=-1), ctx_1024, ctx_1024, L1_xattn_Wq, L1_xattn_bq, L1_xattn_Wk, L1_xattn_bk, L1_xattn_Wv, L1_xattn_bv, L1_xattn_Wo, L1_xattn_bo)
    x = x + _L1_ffn_ref(_layernorm(x, axis=-1), L1_ffn_router_w, L1_ffn_router_b, L1_ffn_expert_w)
    return x

_drawn_inputs = setup_inputs


def setup_inputs(seed=0):
    import zlib

    import numpy as np

    out = dict(_drawn_inputs(seed))
    spreads = {'L0_ffn_ln1_w': (1.0, 0.2),
     'L0_ffn_ln1_b': (0.0, 0.274),
     'L0_ffn_ln2_w': (1.0, 0.2),
     'L0_ffn_ln2_b': (0.0, 0.1),
     'L0_ffn_bqkv': (0.0, 0.1),
     'L0_ffn_bo': (0.0, 0.1),
     'L0_ffn_fc1_b': (0.0, 0.272),
     'L0_ffn_fc2_b': (0.0, 0.1),
     'L1_xattn_bq': (0.0, 0.8),
     'L1_xattn_bk': (0.0, 0.8),
     'L1_xattn_bv': (0.0, 0.1),
     'L1_xattn_bo': (0.0, 0.1)}
    factors = {'L0_xattn_bk': 8.0, 'L1_xattn_Wq': 8.0, 'L1_xattn_Wk': 8.0}
    for name, (base, spread) in spreads.items():
        noise = np.random.default_rng([zlib.crc32(name.encode()), seed]).standard_normal(out[name].shape)
        drawn = base * np.exp(spread * noise) if base else spread * noise
        out[name] = jnp.asarray(drawn.astype(out[name].dtype))
    for name, factor in factors.items():
        out[name] = (out[name] * factor).astype(out[name].dtype)
    return out
```

```python
from contextlib import ExitStack

import concourse.bass as bass
from concourse import mybir

ALU = mybir.AluOpType
ACT = mybir.ActivationFunctionType
AX = mybir.AxisListType
F32 = mybir.dt.float32
F32R = mybir.dt.float32r
BF16 = mybir.dt.bfloat16

P = 128
D = 256
DK = D // P
B, S = 4, 512
T = B * S
TB = T // P
RT = S // P
H0, DH0 = 16, 16
HG = P // DH0
HH = H0 // HG
IT = P // HG
NT0 = S // IT
VW0 = DH0 + 1
ERW = S + 16
E0, F0 = 8, 1024
FK = F0 // P
H1, DH1 = 16, 64
HP = H1 // 2
IT1 = P // 2
VW1 = DH1 + 1
E1 = 16
TOP0, TOP1 = 2, 6
LN_EPS = 1e-5
EPS = 1e-10
LOW = -3e38

COLS = {}
_at = 0
for _name, _n in [("bq0", 2), ("bk0", 2), ("ln1w", 2), ("ln1b", 2), ("ln2w", 2), ("ln2b", 2), ("bqkv", 6),
                  ("bq1", HP), ("bk1", HP)]:
    COLS[_name] = _at
    _at += _n
NCOLS = _at


def build(nc, A, out):
    with ExitStack() as ctx:
        sem = lambda name: ctx.enter_context(nc.semaphore(name))

        base = nc.sbuf_base + 31 & ~31
        at = [base]

        def region(nbytes):
            o = at[0]
            at[0] += nbytes + 31 & ~31
            assert at[0] <= nc.sbuf_usable_end, at[0]
            return o

        def place(name, shape, dt, o=None):
            n = 1
            for s in shape[1:]:
                n *= s
            nbytes = n * (2 if dt == BF16 else 4)
            return nc.alloc_sbuf_tensor_at(name, shape, dt, offset=region(nbytes) if o is None else o)

        KB = 1024
        X = place("X", [P, TB, D], F32)
        NT = place("NT", [P, DK, T], F32)
        rKT = region(16 * KB)
        rVE = region(TB * H0 * VW0 * 4)
        rR1 = region(32 * KB)
        rQB = region(32 * KB)
        rPT = region(28 * KB)
        Pb = place("Pb", [P, 4, S], F32)
        rW0 = region(6 * KB)
        rWF = region(8 * KB)
        rQS = region(8 * KB)
        nrm = place("nrm", [P, 4, D], F32)
        KT = place("KT", [P, HH, T], F32, rKT)
        VE = place("VE", [P, TB, H0, VW0], F32, rVE)
        RB = place("RB", [P, HH, NT0 * 2, 8, HG], F32, rR1)
        CT0 = place("CT0", [P, DK, T], F32, rR1)
        Hs = place("Hs", [P, TB, D], F32, rR1)
        ON = place("ON", [P, TB, D], F32, rR1 + 16 * KB)
        QB = place("QB", [P, HH, S, HG], F32, rQB)
        PT = [place("PT0", [P, 3, 8, P], F32, rPT), place("PT1", [P, 4, 8, P], F32, rPT + 12 * KB)]
        ErS = place("ErS", [P, ERW], F32)
        W0 = place("W0", [P, 3, DK, D], F32, rW0)
        WF = place("WF", [P, DK, 3 * D], F32, rWF)
        WO = place("WO", [P, DK, D], F32, rWF + 6 * KB)
        qhi = place("qhi", [P, S], F32R, rQS)
        qlo = place("qlo", [P, S], F32R, rQS + 2 * KB)
        sel = place("sel", [P, HG, P], F32R, rQS + 4 * KB)
        sel_f = place("sel_f", [P, HG, P], F32, rQB)
        mask_f = place("mask_f", [P, 8, P], F32, rQB + 4 * KB)
        W1b = [place(f"W1b{i}", [P, DK, F0], F32, rQB + 16 * KB * i) for i in range(2)]
        W2b = [place(f"W2b{i}", [P, FK, D], F32, rQB + 16 * KB * i + 8 * KB) for i in range(2)]
        B1b = [place(f"B1b{i}", [P, FK], F32) for i in range(2)]
        hT = [place("hT0", [P, FK, S], F32, rPT), place("hT1", [P, FK, S], F32, rVE)]
        W1 = place("W1", [P, 3, DK, H1 * DH1], F32, rR1)
        WO1 = place("WO1", [P, 8, D], F32, rR1 + 24 * KB)
        CTb = place("CTb", [P, DK, S], F32, rKT)
        K1 = place("K1", [P, HP, S], F32, rQB)
        O1 = place("O1", [P, RT, H1 * DH1], F32, rQB + 16 * KB)
        V1 = place("V1", [P, RT, H1, VW1], F32, rVE)
        QB1 = [place(f"QB1{i}", [P, S, 2], F32, rPT + 4 * KB * i) for i in range(2)]
        PT1 = [place(f"PTb{i}", [P, RT, 2 * P], F32, rPT + 8 * KB + 4 * KB * i) for i in range(2)]
        O1T = [place(f"O1T{i}", [P, 8, P], F32, rPT + 16 * KB + 4 * KB * i) for i in range(2)]
        rows1 = place("rows1", [P, H1 * DH1 + D], F32, rW0)
        WE = place("WE", [P, DK, E1, D], F32, rQB)
        RW = place("RW", [P, DK, E1], F32)
        GW = place("GW", [P, DK, E0], F32)
        fc2b = place("fc2b", [E0, D], F32)
        rb_row = place("rb_row", [P, E1], F32)

        idf = place("idf", [P, P], F32)
        idb = place("idb", [P, P], BF16)
        maskb = place("maskb", [P, 8, P], BF16)
        hm4 = place("hm4", [P, HG], F32)
        hm8 = place("hm8", [P, 2], F32)
        cols = place("cols", [P, NCOLS], F32)
        rows0 = place("rows0", [P, 3, D], F32)
        st = place("st", [P, TB, 6], F32)
        mv = place("mv", [P, TB, 2], F32)
        sd = place("sd", [P, TB], F32)
        rstd = place("rstd", [P, TB], F32)
        nm = place("nm", [P, 8], F32)
        rec = place("rec", [P, 8], F32)
        tmp = place("tmp", [P, P], F32)
        eps_c = place("eps_c", [P, 1], F32)
        lg = place("lg", [P, TB, E1 + 8], F32)
        lg2 = place("lg2", [P, TB, E1 + 8], F32)
        top = place("top", [P, TB, 8], F32)
        gat = place("gat", [P, TB, E1], F32)
        gA = place("gA", [P, TB], F32)
        gB = place("gB", [P, TB], F32)
        gC = place("gC", [P, TB], F32)
        gT = place("gT", [E0, TB, P], F32, rPT)

        PS = [ctx.enter_context(nc.psum_tensor(f"PS{i}", [P, 512], F32)) for i in range(8)]
        SC, TR, OB, G = PS[0:3], PS[3:5], PS[5], PS[6:8]

        ld = {k: sem("ld_" + k) for k in
              ("ctx0", "w0", "const", "x", "er", "wf", "late", "w1", "ctx1", "rows1", "we")}
        s_er0 = sem("s_er0")
        s_init = sem("s_init")
        s_eps = sem("s_eps")
        g_full = [sem(f"g_full{i}") for i in range(2)]
        g_free = [sem(f"g_free{i}") for i in range(2)]
        chain = sem("dve_chain")
        s_out = sem("s_out")

        PER1 = 16 + HP + 3 * RT
        WO_AT = 16 + HP
        USE, N_USE = {}, {}
        n_use = 0
        for name, n in [("kv0", 24), ("ln0", TB), ("q0", B * 2 * (1 + HG)), ("ln1", TB), ("kvf", 24), ("qf", 2 * B),
                        ("ont", TB), ("wo", TB), ("ln2", TB), ("rt0", 1), ("gt", 4), ("ln3", TB),
                        ("p1", B * PER1), ("ln4", TB), ("rt1", 1)]:
            USE[name], N_USE[name] = n_use, n
            n_use += n

        def slot(name, j, b=0, per=0):
            u = USE[name] + j
            return u % 2, u // 2 + b * (per // 2)

        def bank_for_write(eng, name, j, b=0, per=0):
            i, k = slot(name, j, b, per)
            eng.wait_ge(g_free[i], k)
            return G[i]

        def wrote(ins, name, j):
            ins.then_inc(g_full[slot(name, j)[0]], 1)

        def bank_for_read(eng, name, j, b=0, per=0):
            i, k = slot(name, j, b, per)
            eng.wait_ge(g_full[i], k + 1)
            return G[i]

        def has_read(ins, name, j):
            ins.then_inc(g_free[slot(name, j)[0]], 1)

        def wait_stored(eng, name, j, b=0, per=0):
            i, k = slot(name, j, b, per)
            eng.wait_ge(g_free[i], k + 1)

        def wait_all_stored(eng, name):
            u = USE[name] + N_USE[name]
            for i in range(2):
                eng.wait_ge(g_free[i], (u + 1 - i) // 2)

        ln_sem = {t: {k: sem(f"ln{t}_{k}") for k in ("var", "sd", "nrm")} for t in range(5)}
        ln_sem["h"] = {k: sem(f"lnh_{k}") for k in ("var", "sd", "nrm")}

        class AttnSems:
            def __init__(self, tag):
                self.sc = sem(tag + "_scores")
                self.nm = sem(tag + "_negmax")
                self.ex = sem(tag + "_exp")
                self.tr = sem(tag + "_transposed")
                self.pt = sem(tag + "_pt")
                self.pv = sem(tag + "_pv")
                self.rc = sem(tag + "_recip")
                self.mu = sem(tag + "_norm")
                self.o = sem(tag + "_out")
        at0, atf, at1 = AttnSems("a0"), AttnSems("af"), AttnSems("a1")
        s_qhi = sem("qhi")
        s_hb = sem("hs_plus_bias")
        s_xh = sem("x_plus_hs")
        s_xb = sem("x_plus_bo1")
        s_gate = sem("gates")
        s_e = {k: sem("moe0_" + k) for k in ("h", "hT", "y", "x")}
        s_ew = [sem(f"moe0_weights{i}") for i in range(2)]
        s_rt = {k: sem("router_" + k) for k in ("in0", "exp0", "in1", "exp1")}
        s_y1 = sem("moe1_y")
        s_m1 = sem("moe1_acc")
        SUMS = [(0, 0)]
        for tb in range(1, TB):
            SUMS += [(tb, 0), (tb - 1, 1)]
        SUMS += [(TB - 1, 1)]

        block = ctx.enter_context(nc.Block())

        @block.sync
        def _(sp):
            sp.dma_start(CT0[:], A["ctxT"].rearrange("(k p) t -> p k t", p=P)).then_inc(ld["ctx0"], 16)
            for i, w in enumerate(("wq0T", "wk0T", "wv0T")):
                sp.dma_start(W0[:, i], A[w].rearrange("(k p) n -> p k n", p=P)).then_inc(ld["w0"], 16)
            for dst, src in ((cols[:], A["cols"]), (idf[:], A["ident"]), (hm4[:], A["hm4"]), (hm8[:], A["hm8"]),
                             (sel_f[:], A["sel"]), (mask_f[:], A["maskc"])):
                sp.dma_start(dst, src).then_inc(ld["const"], 16)
            for i, r in enumerate(("bv0", "bvf", "bof")):
                sp.dma_start(rows0[:, i], A[r].partition_broadcast(P)).then_inc(ld["const"], 16)
            sp.dma_start(X[:], A["x"].rearrange("(t p) d -> p t d", p=P)).then_inc(ld["x"], 16)
            sp.wait_ge(s_er0, 1)
            for g in range(HG):
                sp.dma_start(ErS[DH0 * g:DH0 * g + DH0, g:g + S], A["ErT"]).then_inc(ld["er"], 16)
            sp.dma_start(WF[:], A["wqkv"].rearrange("(k p) n -> p k n", p=P)).then_inc(ld["wf"], 16)
            sp.dma_start(WO[:], A["wo"].rearrange("(k p) n -> p k n", p=P)).then_inc(ld["wf"], 16)
            sp.dma_start(GW[:], A["gate_w"].rearrange("(k p) n -> p k n", p=P)).then_inc(ld["late"], 16)
            sp.dma_start(RW[:], A["rwT"].rearrange("(k p) n -> p k n", p=P)).then_inc(ld["late"], 16)
            sp.dma_start(fc2b[:], A["fc2b"]).then_inc(ld["late"], 16)
            sp.dma_start(rb_row[:], A["rb"].partition_broadcast(P)).then_inc(ld["late"], 16)

            def expert_weights(e, i):
                sp.dma_start(W1b[i][:], A["fc1T"][e].rearrange("(k p) f -> p k f", p=P)).then_inc(s_ew[i], 16)
                sp.dma_start(B1b[i][:], A["fc1b"][e]).then_inc(s_ew[i], 16)
                sp.dma_start(W2b[i][:], A["fc2T"][e].rearrange("(k p) d -> p k d", p=P)).then_inc(s_ew[i], 16)

            sp.wait_ge(atf.sc, B * 64)
            expert_weights(0, 0)
            expert_weights(1, 1)

            def context(b):
                sp.dma_start(CTb[:], A["ctxT"].rearrange("(k p) t -> p k t", p=P)[:, :, bass.ds(b * S, S)])\
                    .then_inc(ld["ctx1"], 16)

            context(0)
            wait_all_stored(sp, "wo")
            sp.dma_start(rows1[:, 0:H1 * DH1], A["bv1"].partition_broadcast(P)).then_inc(ld["rows1"], 16)
            sp.dma_start(rows1[:, H1 * DH1:], A["bo1"].partition_broadcast(P)).then_inc(ld["rows1"], 16)
            sp.wait_ge(s_xh, TB)
            sp.wait_ge(ln_sem[2]["nrm"], TB)
            for i, w in enumerate(("wq1", "wk1", "wv1")):
                sp.dma_start(W1[:, i], A[w].rearrange("(k p) n -> p k n", p=P)).then_inc(ld["w1"], 16)
            sp.dma_start(WO1[:], A["wo1"].rearrange("(k p) n -> p k n", p=P)).then_inc(ld["w1"], 16)
            for e in range(2, E0):
                sp.wait_ge(s_e["y"], 16 * (e - 1) + TB)
                expert_weights(e, e % 2)
            i, k = slot("p1", 15)
            with sp.Fori(1, B) as b:
                sp.wait_ge(g_full[i], b * (PER1 // 2) + k + 1 - PER1 // 2)
                context(b)
            i, k = slot("p1", B * PER1 - 1)
            sp.wait_ge(g_full[i], k + 1)
            for k in range(DK):
                sp.dma_start(WE[:, k], A["we"][:, k * P:k * P + P, :].rearrange("e p n -> p e n")).then_inc(ld["we"], 16)
            sp.wait_ge(s_m1, TB * E1 + 2 * TB)
            for i in range(4):
                sp.dma_start(out.rearrange("(t p) d -> p t d", p=P)[:, 4 * i:4 * i + 4], X[:, 4 * i:4 * i + 4])\
                    .then_inc(s_out, 16)
            sp.wait_ge(s_out, 64)

        @block.gpsimd
        def _(pool):
            nc.gpsimd.memset(ErS[:], 0.0).then_inc(s_er0, 1)
            nc.gpsimd.memset(eps_c[:], LN_EPS).then_inc(s_eps, 1)
            pool.wait_ge(ld["const"], 16 * 9)
            for tb in range(TB):
                pool.wait_ge(ln_sem[1]["nrm"], tb + 1)
                nc.gpsimd.tensor_tensor(Hs[:, tb], Hs[:, tb], rows0[:, 2], ALU.add).then_inc(s_hb, 1)
            for tb in range(TB):
                wait_stored(pool, "wo", tb)
                nc.gpsimd.tensor_tensor(X[:, tb], X[:, tb], Hs[:, tb], ALU.add).then_inc(s_xh, 1)
            pool.wait_ge(ld["rows1"], 32)
            for tb in range(TB):
                pool.wait_ge(ln_sem[3]["nrm"], tb + 1)
                nc.gpsimd.tensor_tensor(X[:, tb], X[:, tb], rows1[:, H1 * DH1:], ALU.add).then_inc(s_xb, 1)

        @block.tensor
        def _(pe):
            mm = nc.tensor.matmul

            def project(bank, w, src, n, m=P):
                for k in range(DK):
                    last = mm(bank[0:m, 0:n], w(k), src(k), start=(k == 0), stop=(k == DK - 1))
                return last

            def keys_values(name, wk, wv, src_k, src_v):
                for hh in range(HH):
                    for b in range(B):
                        j = hh * B + b
                        bank = bank_for_write(pe, name, j)
                        wrote(project(bank, lambda k: wk(k, hh), lambda k: src_k(k, b), S), name, j)
                for tb in range(TB):
                    j = 8 + tb
                    bank = bank_for_write(pe, name, j)
                    wrote(project(bank, lambda k: src_v(k, tb), wv, D), name, j)

            def ln_transposes(t, name, src):
                for tb in range(TB):
                    bank = bank_for_write(pe, name, tb)
                    pe.wait_ge(ln_sem[t]["nrm"], tb + 1)
                    for k in range(DK):
                        last = nc.tensor.transpose(bank[:, k * P:k * P + P], src(tb)[:, k * P:k * P + P], idf[:])
                    wrote(last, name, tb)

            def attention0(a, b, rel):
                def scores(n):
                    hh, t = divmod(n, NT0)
                    if t == 0:
                        if rel:
                            wait_stored(pe, "q0", hh * (1 + HG) + HG, b, HH * (1 + HG))
                            wait_stored(pe, "q0", hh * (1 + HG) + HG - 1, b, HH * (1 + HG))
                        else:
                            wait_stored(pe, "qf", hh, b, HH)
                    if n >= 3:
                        pe.wait_ge(a.ex, b * 64 + n - 2)
                    bank, r, w = SC[n % 3], t // 8, IT * (t + 1)
                    mm(bank[:, r * P:r * P + P], idb[:], maskb[:, t % 8, :], start=True, stop=False,
                       skip_group_check=True)
                    last = mm(bank[:, 0:w], QB[:, hh, t * IT:t * IT + IT, :].rearrange("p i h -> p (i h)"),
                              KT[:, hh, bass.ds(b * S, w)], start=False, stop=not rel, skip_group_check=True)
                    for u in range(2 if rel else 0):
                        o = S - 1 - IT * t - 8 * u
                        last = mm(bank[64 * u:64 * u + 64, 0:w],
                                  RB[:, hh, 2 * t + u].rearrange("p i h -> p (i h)"),
                                  ErS[:, o:o + w], start=False, stop=(u == 1), skip_group_check=True)
                    last.then_inc(a.sc, 1)

                def transposes(n):
                    t = n % NT0
                    pe.wait_ge(a.ex, b * 64 + n + 1)
                    if n >= 2:
                        pe.wait_ge(a.pt, b * 64 + n - 1)
                    for c in range(t // 8 + 1):
                        last = nc.tensor.transpose(TR[n % 2][:, c * P:c * P + P], Pb[:, n % 4, c * P:c * P + P],
                                                   idf[:])
                    last.then_inc(a.tr, 1)

                def values(g):
                    hh, r = divmod(g, 4)
                    pe.wait_ge(a.pt, b * 64 + 8 * g + 8)
                    if g:
                        pe.wait_ge(a.mu, b * 8 + g)
                    for h in range(HG):
                        for c in range(r + 1):
                            lhsT = PT[g % 2][:, c].rearrange("p s (i h) -> p (s i) h", h=HG)[:, :, h]
                            rhs = VE[:, bass.ds(b * RT + c, 1), hh * HG + h, :]
                            last = mm(OB[:, h * VW0:h * VW0 + VW0], lhsT, rhs,
                                      start=(c == 0), stop=(c == r), skip_group_check=True)
                    last.then_inc(a.pv, 1)

                for n in range(64 + 4):
                    if n < 64:
                        scores(n)
                    if 2 <= n < 66:
                        transposes(n - 2)
                    if n >= 11 and (n - 11) % 8 == 0:
                        values((n - 11) // 8)

            pe.wait_ge(ld["ctx0"], 16)
            pe.wait_ge(ld["w0"], 48)
            keys_values("kv0", lambda k, hh: W0[:, 1, k, hh * P:hh * P + P], lambda k: W0[:, 2, k, :],
                        lambda k, b: CT0[:, k, b * S:b * S + S], lambda k, tb: CT0[:, k, tb * P:tb * P + P])
            pe.wait_ge(ld["const"], 16 * 9)
            ln_transposes(0, "ln0", lambda tb: nrm[:, tb % 4])
            pe.wait_ge(ld["er"], 16 * HG)
            pe.wait_ge(s_init, 5)
            with pe.Fori(0, B) as b:
                for hh in range(HH):
                    per = 2 * (1 + HG)
                    j = hh * (1 + HG)
                    bank = bank_for_write(pe, "q0", j, b, per)
                    wrote(project(bank, lambda k: W0[:, 0, k, hh * P:hh * P + P],
                                  lambda k: NT[:, k, bass.ds(b * S, S)], S), "q0", j)
                    pe.wait_ge(s_qhi, b * HH + hh + 1)
                    wait_stored(pe, "q0", j, b, per)
                    for h in range(HG):
                        bank = bank_for_write(pe, "q0", j + 1 + h, b, per)
                        mm(bank[:], sel[:, h], qhi[:], start=True, stop=False)
                        wrote(mm(bank[:], sel[:, h], qlo[:], start=False, stop=True), "q0", j + 1 + h)
                attention0(at0, b, True)

            ln_transposes(1, "ln1", lambda tb: nrm[:, tb % 4])
            pe.wait_ge(ld["wf"], 32)
            wait_all_stored(pe, "ln1")
            keys_values("kvf", lambda k, hh: WF[:, k, D + hh * P:D + hh * P + P], lambda k: WF[:, k, 2 * D:3 * D],
                        lambda k, b: NT[:, k, b * S:b * S + S], lambda k, tb: NT[:, k, tb * P:tb * P + P])
            with pe.Fori(0, B) as b:
                for hh in range(HH):
                    bank = bank_for_write(pe, "qf", hh, b, 2)
                    wrote(project(bank, lambda k: WF[:, k, hh * P:hh * P + P],
                                  lambda k: NT[:, k, bass.ds(b * S, S)], S), "qf", hh)
                attention0(atf, b, False)
            for tb in range(TB):
                bank = bank_for_write(pe, "ont", tb)
                pe.wait_ge(atf.mu, 8 * (tb // 4) + 5 + tb % 4)
                for k in range(DK):
                    last = nc.tensor.transpose(bank[:, k * P:k * P + P], ON[:, tb, k * P:k * P + P], idf[:])
                wrote(last, "ont", tb)
            for tb in range(TB):
                bank = bank_for_write(pe, "wo", tb)
                wait_stored(pe, "ont", tb)
                wrote(project(bank, lambda k: NT[:, k, tb * P:tb * P + P], lambda k: WO[:, k, :], D), "wo", tb)
            ln_transposes(2, "ln2", lambda tb: nrm[:, tb % 4])

            pe.wait_ge(ld["late"], 64)
            wait_all_stored(pe, "ln2")
            bank = bank_for_write(pe, "rt0", 0)
            for tb in range(TB):
                for k in range(DK):
                    last = mm(bank[:, tb * E0:tb * E0 + E0], NT[:, k, tb * P:tb * P + P], GW[:, k, :],
                              start=(k == 0), stop=(k == DK - 1), skip_group_check=True)
            wrote(last, "rt0", 0)
            pe.wait_ge(s_gate, 1)
            for i in range(4):
                bank = bank_for_write(pe, "gt", i)
                for q in range(4):
                    last = nc.tensor.transpose(bank[0:E0, q * P:q * P + P], gat[:, i * 4 + q, 0:E0], idf[:])
                wrote(last, "gt", i)
            wait_all_stored(pe, "gt")
            for tb in range(TB):
                if tb >= 4:
                    pe.wait_ge(s_e["x"], tb - 3)
                mm(PS[4 + tb % 4][:, 0:D], gT[:, tb, :], fc2b[:], start=True, stop=True).then_inc(s_e["y"], 1)

            def up(ep, s):
                e, c = divmod(s, 4)
                if c == 0:
                    pe.wait_ge(s_ew[e], ep * 48 + 48)
                for f in range(FK):
                    if s or f >= 4:
                        pe.wait_ge(s_e["hT"], ep * 64 + s * FK + f - 3)
                    last = project(PS[f % 4], lambda k: W1b[e][:, k, f * P:f * P + P],
                                   lambda k: NT[:, k, c * S:c * S + S], S)
                    last.then_inc(s_e["h"], 1)

            def down(ep, s):
                e, c = divmod(s, 4)
                pe.wait_ge(s_e["hT"], ep * 64 + s * FK + 8)
                for q in range(4):
                    pe.wait_ge(s_e["x"], ep * 32 + TB + s * 4 + q - 3)
                    for f in range(FK):
                        last = mm(PS[4 + q][:, 0:D], hT[s % 2][:, f, q * P:q * P + P], W2b[e][:, f, :],
                                  start=(f == 0), stop=(f == FK - 1))
                    last.then_inc(s_e["y"], 1)

            with pe.Fori(0, E0 // 2) as ep:
                for s in range(9):
                    if s < 8:
                        up(ep, s)
                    if s >= 1:
                        down(ep, s - 1)

            pe.wait_ge(s_e["x"], 16 * E0 + TB)
            ln_transposes(3, "ln3", lambda tb: nrm[:, tb % 4])
            wait_all_stored(pe, "ln3")
            pe.wait_ge(ld["w1"], 64)
            with pe.Fori(0, B) as b:
                pe.wait_ge(ld["ctx1"], b * 16 + 16)
                for m in range(HP):
                    bank = bank_for_write(pe, "p1", m, b, PER1)
                    wrote(project(bank, lambda k: W1[:, 1, k, m * P:m * P + P],
                                  lambda k: CTb[:, k, :], S), "p1", m)
                for r in range(RT):
                    for hf in range(2):
                        j = HP + 2 * r + hf
                        bank = bank_for_write(pe, "p1", j, b, PER1)
                        wrote(project(bank, lambda k: CTb[:, k, r * P:r * P + P],
                                      lambda k: W1[:, 2, k, hf * S:hf * S + S], S), "p1", j)

                def queries(p):
                    bank = bank_for_write(pe, "p1", 16 + p, b, PER1)
                    wrote(project(bank, lambda k: W1[:, 0, k, p * P:p * P + P],
                                  lambda k: NT[:, k, bass.ds(b * S, S)], S), "p1", 16 + p)

                def scores(n):
                    p, it = divmod(n, 8)
                    if it == 0:
                        wait_stored(pe, "p1", 16 + p, b, PER1)
                    if n >= 3:
                        pe.wait_ge(at1.ex, b * 64 + n - 2)
                    mm(SC[n % 3][:], QB1[p % 2][:, it * IT1:it * IT1 + IT1, :].rearrange("p i h -> p (i h)"),
                       K1[:, p, :], start=True, stop=True).then_inc(at1.sc, 1)

                def transposes(n):
                    pe.wait_ge(at1.ex, b * 64 + n + 1)
                    if n >= 2:
                        pe.wait_ge(at1.pt, b * 64 + n - 1)
                    for c in range(RT):
                        last = nc.tensor.transpose(TR[n % 2][:, c * P:c * P + P], Pb[:, n % 4, c * P:c * P + P],
                                                   idf[:])
                    last.then_inc(at1.tr, 1)

                def values(g):
                    p, r = divmod(g, 4)
                    pe.wait_ge(at1.pt, b * 64 + 2 * g + 2)
                    if g:
                        pe.wait_ge(at1.mu, b * 32 + g)
                    for h in range(2):
                        for c in range(RT):
                            lhsT = PT1[g % 2][:, c].rearrange("p (i h) -> p i h", h=2)[:, :, h]
                            last = mm(OB[:, h * VW1:h * VW1 + VW1], lhsT, V1[:, c, 2 * p + h, :],
                                      start=(c == 0), stop=(c == RT - 1), skip_group_check=True)
                    last.then_inc(at1.pv, 1)

                wait_stored(pe, "p1", 14, b, PER1)
                wait_stored(pe, "p1", 15, b, PER1)
                queries(0)
                for n in range(64 + 4):
                    if n < 64:
                        if n % 8 == 2 and n < 58:
                            queries(n // 8 + 1)
                        scores(n)
                    if 2 <= n < 66:
                        transposes(n - 2)
                    if n >= 5 and (n - 5) % 2 == 0:
                        values((n - 5) // 2)
                for r in range(RT):
                    pe.wait_ge(at1.mu, b * 32 + 29 + r)
                    for hf in range(2):
                        j = WO_AT + 3 * r + hf
                        bank = bank_for_write(pe, "p1", j, b, PER1)
                        for k in range(4):
                            kk = hf * 4 + k
                            last = nc.tensor.transpose(bank[:, k * P:k * P + P], O1[:, r, kk * P:kk * P + P], idf[:])
                        wrote(last, "p1", j)
                    j = WO_AT + 3 * r + 2
                    bank = bank_for_write(pe, "p1", j, b, PER1)
                    wait_stored(pe, "p1", j - 2, b, PER1)
                    wait_stored(pe, "p1", j - 1, b, PER1)
                    for k in range(8):
                        last = mm(bank[:, 0:D], O1T[r % 2][:, k, :], WO1[:, k, :], start=(k == 0), stop=(k == 7))
                    wrote(last, "p1", j)

            ln_transposes(4, "ln4", lambda tb: nrm[:, tb % 4])
            wait_all_stored(pe, "ln4")
            bank = bank_for_write(pe, "rt1", 0)
            for tb in range(TB):
                for k in range(DK):
                    last = mm(bank[:, tb * E1:tb * E1 + E1], NT[:, k, tb * P:tb * P + P], RW[:, k, :],
                              start=(k == 0), stop=(k == DK - 1), skip_group_check=True)
            wrote(last, "rt1", 0)
            pe.wait_ge(ld["we"], 16 * DK)
            with pe.Fori(0, E1 // 2) as ep:
                for tb in range(TB):
                    read = SUMS.index(((tb - 8) % TB, 1)) + 1 + (0 if tb < 8 else 2 * TB)
                    pe.wait_ge(s_m1, ep * (2 * TB) + read)
                    last = project(PS[tb % 8], lambda k: NT[:, k, tb * P:tb * P + P],
                                   lambda k: WE[:, k, bass.ds(2 * ep, 2), :].rearrange("p e n -> p (e n)"), 2 * D)
                    last.then_inc(s_y1, 1)

        @block.scalar
        def _(act):
            af = nc.scalar.activation

            def ln_part(t, name, w=None, bcol=None, transposed=True):
                act.wait_ge(ln_sem[t]["var"], 1)
                af(sd[:], mv[:, :, 1], ACT.Sqrt, bias=eps_c[:, 0:1]).then_inc(ln_sem[t]["sd"], 1)
                for tb in range(TB if transposed else 0):
                    bank = bank_for_read(act, name, tb)
                    for k in range(DK):
                        if w is None:
                            last = af(NT[:, k, tb * P:tb * P + P], bank[:, k * P:k * P + P], ACT.Identity)
                        else:
                            last = af(NT[:, k, tb * P:tb * P + P], bank[:, k * P:k * P + P], ACT.Identity,
                                      scale=cols[:, w + k:w + k + 1], bias=cols[:, bcol + k:bcol + k + 1])
                    has_read(last, name, tb)

            def keys(name, bcol):
                for hh in range(HH):
                    for b in range(B):
                        bank = bank_for_read(act, name, hh * B + b)
                        ins = af(KT[:, hh, b * S:b * S + S], bank[:], ACT.Identity,
                                 bias=cols[:, bcol + hh:bcol + hh + 1])
                        has_read(ins, name, hh * B + b)
                        
            def attention0(a, b):
                for n in range(64 + 2):
                    if n < 64:
                        t = n % NT0
                        act.wait_ge(a.nm, b * 64 + n + 1)
                        if n >= 4:
                            act.wait_ge(a.tr, b * 64 + n - 3)
                        w = P * (t // 8 + 1)
                        af(Pb[:, n % 4, 0:w], SC[n % 3][:, 0:w], ACT.Exp, bias=nm[:, n % 8:n % 8 + 1])\
                            .then_inc(a.ex, 1)
                    if n >= 2:
                        m = n - 2
                        t, g = m % NT0, m // 8
                        act.wait_ge(a.tr, b * 64 + m + 1)
                        if m % 8 == 0 and g >= 2:
                            act.wait_ge(a.pv, b * 8 + g - 1)
                        c = t // 8 + 1
                        af(PT[g % 2][:, 0:c, m % 8, :], TR[m % 2][:, 0:c * P].rearrange("p (c q) -> p c q", c=c),
                           ACT.Copy).then_inc(a.pt, 1)

            act.wait_ge(ld["const"], 16 * 9)
            keys("kv0", COLS["bk0"])
            act.wait_ge(s_eps, 1)
            ln_part(0, "ln0")
            with act.Fori(0, B) as b:
                for hh in range(HH):
                    per = 2 * (1 + HG)
                    j = hh * (1 + HG)
                    bank = bank_for_read(act, "q0", j, b, per)
                    wait_stored(act, "q0", j - 1, b, per)
                    af(qhi[:], bank[:], ACT.Identity, bias=cols[:, COLS["bq0"] + hh:COLS["bq0"] + hh + 1])\
                        .then_inc(s_qhi, 1)
                attention0(at0, b)
            ln_part("h", None, transposed=False)
            ln_part(1, "ln1", COLS["ln1w"], COLS["ln1b"])
            keys("kvf", COLS["bqkv"] + 2)
            with act.Fori(0, B) as b:
                attention0(atf, b)
            for tb in range(TB):
                bank = bank_for_read(act, "ont", tb)
                has_read(af(NT[:, :, tb * P:tb * P + P], bank[:, 0:D].rearrange("p (k q) -> p k q", k=DK),
                            ACT.Copy), "ont", tb)
            ln_part(2, "ln2", COLS["ln2w"], COLS["ln2b"])
            act.wait_ge(s_rt["in0"], 1)
            af(lg2[:, :, 0:E0], lg2[:, :, 0:E0], ACT.Exp).then_inc(s_rt["exp0"], 1)
            for i in range(4):
                bank = bank_for_read(act, "gt", i)
                has_read(af(gT[:, i * 4:i * 4 + 4, :], bank[0:E0, :].rearrange("p (q c) -> p q c", q=4), ACT.Copy),
                         "gt", i)
            with act.Fori(0, E0 // 2) as ep:
                for s in range(8):
                    for f in range(FK):
                        act.wait_ge(s_e["h"], ep * 64 + s * FK + f + 1)
                        if f == 0:
                            act.wait_ge(s_e["y"], ep * 32 + TB + 4 * (s - 1))
                        af(hT[s % 2][:, f, :], PS[f % 4][:], ACT.Gelu,
                           bias=B1b[s // 4][:, f:f + 1])\
                            .then_inc(s_e["hT"], 1)
            ln_part(3, "ln3")
            with act.Fori(0, B) as b:
                for m in range(HP):
                    bank = bank_for_read(act, "p1", m, b, PER1)
                    ins = af(K1[:, m, :], bank[:], ACT.Identity,
                             bias=cols[:, COLS["bk1"] + m:COLS["bk1"] + m + 1])
                    has_read(ins, "p1", m)
                for n in range(64 + 2):
                    if n < 64:
                        act.wait_ge(at1.nm, b * 64 + n + 1)
                        if n >= 4:
                            act.wait_ge(at1.tr, b * 64 + n - 3)
                        af(Pb[:, n % 4, :], SC[n % 3][:], ACT.Exp, bias=nm[:, n % 8:n % 8 + 1]).then_inc(at1.ex, 1)
                    if n >= 2:
                        m = n - 2
                        g = m // 2
                        act.wait_ge(at1.tr, b * 64 + m + 1)
                        if m % 2 == 0 and g >= 2:
                            act.wait_ge(at1.pv, b * 32 + g - 1)
                        af(PT1[g % 2][:, :, (m % 2) * P:(m % 2) * P + P], TR[m % 2][:].rearrange("p (c q) -> p c q", c=RT),
                           ACT.Copy).then_inc(at1.pt, 1)
                for r in range(RT):
                    for hf in range(2):
                        j = WO_AT + 3 * r + hf
                        bank = bank_for_read(act, "p1", j, b, PER1)
                        has_read(af(O1T[r % 2][:, hf * 4:hf * 4 + 4, :], bank[:].rearrange("p (k q) -> p k q", k=4),
                                    ACT.Copy), "p1", j)
            ln_part(4, "ln4")
            act.wait_ge(s_rt["in1"], 1)
            af(lg2[:, :, 0:E1], lg2[:, :, 0:E1], ACT.Exp).then_inc(s_rt["exp1"], 1)

        @block.vector
        def _(dve):
            v = nc.vector
            done = [0]

            def link(ins):
                done[0] += 1
                ins.then_inc(chain, 1)
                dve.wait_ge(chain, done[0])

            def ln_part(t, name, src, dst, ready=None):
                for tb in range(TB):
                    if ready:
                        ready(tb)
                    last = v.bn_stats(st[:, tb, :], src(tb))
                link(last)
                for tb in range(TB):
                    last = v.bn_aggr(mv[:, tb, :], st[:, tb, :])
                last.then_inc(ln_sem[t]["var"], 1)
                dve.wait_ge(ln_sem[t]["sd"], 1)
                link(v.reciprocal(rstd[:], sd[:]))
                for tb in range(TB):
                    if name and tb >= 4:
                        i, k = slot(name, tb - 4)
                        dve.wait_ge(g_full[i], k + 1)
                    v.tensor_scalar(dst(tb), src(tb), mv[:, tb, 0:1], rstd[:, tb:tb + 1], ALU.subtract, ALU.mult)\
                        .then_inc(ln_sem[t]["nrm"], 1)

            def values(name, row):
                for tb in range(TB):
                    bank = bank_for_read(dve, name, 8 + tb)
                    has_read(v.tensor_tensor(VE[:, tb, :, 0:DH0], bank[:, 0:D].rearrange("p (h d) -> p h d", d=DH0),
                                             rows0[:, row].rearrange("p (h d) -> p h d", d=DH0), ALU.add),
                             name, 8 + tb)

            def spread(out, bank, bcol, mask):
                n, m = out.shape[1], out.shape[2]
                return v.scalar_tensor_tensor(out, bank[:].unsqueeze(2).to_broadcast([P, n, m]),
                                              cols[:, bcol:bcol + 1], mask[:].unsqueeze(1).to_broadcast([P, n, m]),
                                              ALU.add, ALU.mult)

            def negmax(a, b, n, w):
                dve.wait_ge(a.sc, b * 64 + n + 1)
                if n >= 8:
                    dve.wait_ge(a.ex, b * 64 + n - 7)
                v.tensor_reduce(nm[:, n % 8:n % 8 + 1], SC[n % 3][:, 0:w], AX.X, ALU.max, negate=True)\
                    .then_inc(a.nm, 1)

            def normalised(a, dst, heads, width, g, b, per):
                dve.wait_ge(a.pv, b * per + g + 1)
                if g:
                    dve.wait_ge(a.mu, b * per + g)
                o = OB[:, 0:heads * width].rearrange("p (h w) -> p h w", w=width)
                v.reciprocal(rec[:, 0:heads], o[:, :, width - 1]).then_inc(a.rc, 1)
                dve.wait_ge(a.rc, b * per + g + 1)
                v.tensor_tensor(dst.rearrange("p (h w) -> p h w", w=width - 1), o[:, :, 0:width - 1],
                                rec[:, 0:heads].unsqueeze(2).to_broadcast([P, heads, width - 1]), ALU.mult)\
                    .then_inc(a.mu, 1)

            def attention0(a, b, to_x):
                def output(g):
                    hh, r = divmod(g, 4)
                    off = (b * RT + r) * D + hh * P
                    if to_x:
                        if g:
                            dve.wait_ge(a.o, b * 8 + g)
                        normalised(a, tmp[:], HG, VW0, g, b, 8)
                        dve.wait_ge(a.mu, b * 8 + g + 1)
                        x = X[:].rearrange("p t d -> p (t d)")[:, bass.ds(off, P)]
                        v.tensor_tensor(x, x, tmp[:], ALU.add).then_inc(a.o, 1)
                    else:
                        normalised(a, ON[:].rearrange("p t d -> p (t d)")[:, bass.ds(off, P)], HG, VW0, g, b, 8)

                for n in range(64):
                    negmax(a, b, n, IT * (n % NT0 + 1))
                    if n >= 12 and (n - 12) % 8 == 0:
                        output((n - 12) // 8)
                output(7)
                dve.wait_ge(a.o if to_x else a.mu, b * 8 + 8)

            v.memset(VE[:, :, :, DH0:VW0], 1.0).then_inc(s_init, 1)
            v.memset(lg[:], LOW).then_inc(s_init, 1)
            dve.wait_ge(ld["const"], 16 * 9)
            v.tensor_copy(idb[:], idf[:]).then_inc(s_init, 1)
            v.tensor_copy(maskb[:], mask_f[:]).then_inc(s_init, 1)
            v.tensor_copy(sel[:], sel_f[:]).then_inc(s_init, 1)
            values("kv0", 0)
            dve.wait_ge(ld["x"], 16)
            dve.wait_ge(s_init, 5)
            ln_part(0, "ln0", lambda tb: X[:, tb], lambda tb: nrm[:, tb % 4])
            with dve.Fori(0, B) as b:
                for hh in range(HH):
                    per = HH * (1 + HG)
                    j = hh * (1 + HG)
                    bank = bank_for_read(dve, "q0", j, b, per)
                    bq = COLS["bq0"] + hh
                    dve.wait_ge(s_qhi, b * HH + hh + 1)
                    spread(QB[:, hh], bank, bq, hm4)
                    has_read(v.scalar_tensor_tensor(qlo[:], bank[:], cols[:, bq:bq + 1], qhi[:].bitcast(F32),
                                                    ALU.add, ALU.subtract), "q0", j)
                    for h in range(HG):
                        bank = bank_for_read(dve, "q0", j + 1 + h, b, per)
                        dst = RB[:, hh].rearrange("p a g h -> p a g h")[:, :, :, h]
                        has_read(v.tensor_tensor(dst, bank[:].rearrange("p (a g) -> p a g", g=8),
                                                 hm4[:].unsqueeze(1).to_broadcast([P, S // 8, 8]), ALU.mult),
                                 "q0", j + 1 + h)
                attention0(at0, b, True)

            dve.wait_ge(at0.o, 8 * B)
            ln_part("h", None, lambda tb: X[:, tb], lambda tb: Hs[:, tb])
            dve.wait_ge(ln_sem["h"]["nrm"], TB)
            ln_part(1, "ln1", lambda tb: Hs[:, tb], lambda tb: nrm[:, tb % 4])
            values("kvf", 1)
            with dve.Fori(0, B) as b:
                for hh in range(HH):
                    bank = bank_for_read(dve, "qf", hh, b, HH)
                    has_read(spread(QB[:, hh], bank, COLS["bqkv"] + hh, hm4), "qf", hh)
                attention0(atf, b, False)
            for tb in range(TB):
                bank = bank_for_read(dve, "wo", tb)
                dve.wait_ge(s_hb, tb + 1)
                has_read(v.tensor_tensor(Hs[:, tb], bank[:, 0:D], Hs[:, tb], ALU.add), "wo", tb)
            ln_part(2, "ln2", lambda tb: Hs[:, tb], lambda tb: nrm[:, tb % 4],
                    ready=lambda tb: wait_stored(dve, "wo", tb))

            def top_mask(width, k):
                for tb in range(TB):
                    last = v.max(top[:, tb, :], lg[:, tb, 0:width + 8])
                link(last)
                link(v.memset(top[:, :, k:8], LOW))
                for tb in range(TB):
                    last = v.match_replace(lg2[:, tb, 0:width + 8], top[:, tb, :], lg[:, tb, 0:width + 8], LOW)
                link(last)
                link(v.tensor_tensor(gat[:, :, 0:width], lg2[:, :, 0:width], lg[:, :, 0:width], ALU.not_equal))

            def over(col, width):
                return col.unsqueeze(2).to_broadcast([P, TB, width])

            bank = bank_for_read(dve, "rt0", 0)
            ins = v.tensor_copy(lg[:, :, 0:E0], bank[:, 0:TB * E0].rearrange("p (t e) -> p t e", e=E0))
            has_read(ins, "rt0", 0)
            wait_stored(dve, "rt0", 0)
            v_max = top[:, :, 0]
            for tb in range(TB):
                last = v.max(top[:, tb, :], lg[:, tb, 0:E0 + 8])
            link(last)
            link(v.tensor_copy(gA[:], v_max))
            top_mask(E0, TOP0)
            v.tensor_tensor(lg2[:, :, 0:E0], lg[:, :, 0:E0], over(gA[:], E0), ALU.subtract).then_inc(s_rt["in0"], 1)
            dve.wait_ge(s_rt["exp0"], 1)
            link(v.tensor_tensor(gat[:, :, 0:E0], gat[:, :, 0:E0], lg2[:, :, 0:E0], ALU.mult))
            link(v.tensor_reduce(gA[:], gat[:, :, 0:E0], AX.X, ALU.add))
            link(v.reciprocal(gB[:], gA[:]))
            ins = v.tensor_tensor(gat[:, :, 0:E0], gat[:, :, 0:E0], over(gB[:], E0), ALU.mult)
            ins.then_inc(s_gate, 1)
            for tb in range(TB):
                dve.wait_ge(s_e["y"], tb + 1)
                dve.wait_ge(s_xh, tb + 1)
                v.tensor_tensor(X[:, tb], PS[4 + tb % 4][:, 0:D], X[:, tb], ALU.add).then_inc(s_e["x"], 1)
            gat_flat = gat[:].rearrange("p t e -> p (t e)")
            with dve.Fori(0, E0 // 2) as ep:
                for s in range(8):
                    for q in range(4):
                        tb = (s % 4) * 4 + q
                        dve.wait_ge(s_e["y"], ep * 32 + TB + s * 4 + q + 1)
                        dve.wait_ge(s_e["x"], ep * 32 + s * 4 + q + 1)
                        v.scalar_tensor_tensor(X[:, tb], PS[4 + q][:, 0:D],
                                               gat_flat[:, bass.ds(2 * ep + tb * E1 + s // 4, 1)], X[:, tb],
                                               ALU.mult, ALU.add).then_inc(s_e["x"], 1)

            dve.wait_ge(s_e["x"], 16 * E0 + TB)
            ln_part(3, "ln3", lambda tb: X[:, tb], lambda tb: nrm[:, tb % 4])
            dve.wait_ge(s_e["y"], 16 * E0 + TB)
            link(v.memset(V1[:, :, :, DH1:VW1], 1.0))
            dve.wait_ge(ld["rows1"], 32)
            with dve.Fori(0, B) as b:
                for r in range(RT):
                    for hf in range(2):
                        j = HP + 2 * r + hf
                        bank = bank_for_read(dve, "p1", j, b, PER1)
                        has_read(v.tensor_tensor(V1[:, r, hf * 8:hf * 8 + 8, 0:DH1],
                                                 bank[:].rearrange("p (h d) -> p h d", d=DH1),
                                                 rows1[:, hf * S:hf * S + S].rearrange("p (h d) -> p h d", d=DH1),
                                                 ALU.add), "p1", j)

                def queries(p):
                    bank = bank_for_read(dve, "p1", 16 + p, b, PER1)
                    has_read(spread(QB1[p % 2][:], bank, COLS["bq1"] + p, hm8), "p1", 16 + p)

                def output(g):
                    p, r = divmod(g, 4)
                    normalised(at1, O1[:, r, p * P:p * P + P], 2, VW1, g, b, 32)

                queries(0)
                for n in range(64):
                    negmax(at1, b, n, S)
                    if n % 8 == 2 and n < 58:
                        queries(n // 8 + 1)
                    if n >= 6 and n % 2 == 0:
                        output((n - 6) // 2)
                for g in range(29, 32):
                    output(g)
                dve.wait_ge(at1.mu, b * 32 + 32)
                for r in range(RT):
                    bank = bank_for_read(dve, "p1", WO_AT + 3 * r + 2, b, PER1)
                    dve.wait_ge(s_xb, TB)
                    x = X[:].rearrange("p t d -> p (t d)")[:, bass.ds((b * RT + r) * D, D)]
                    has_read(v.tensor_tensor(x, bank[:, 0:D], x, ALU.add), "p1", WO_AT + 3 * r + 2)

            wait_all_stored(dve, "p1")
            ln_part(4, "ln4", lambda tb: X[:, tb], lambda tb: nrm[:, tb % 4])

            bank = bank_for_read(dve, "rt1", 0)
            has_read(v.tensor_tensor(lg[:, :, 0:E1], bank[:, 0:TB * E1].rearrange("p (t e) -> p t e", e=E1),
                                     rb_row[:].unsqueeze(1).to_broadcast([P, TB, E1]), ALU.add), "rt1", 0)
            wait_stored(dve, "rt1", 0)
            link(v.tensor_reduce(gA[:], lg[:, :, 0:E1], AX.X, ALU.max))
            v.tensor_tensor(lg2[:, :, 0:E1], lg[:, :, 0:E1], over(gA[:], E1), ALU.subtract).then_inc(s_rt["in1"], 1)
            dve.wait_ge(s_rt["exp1"], 1)
            link(v.tensor_reduce(gA[:], lg2[:, :, 0:E1], AX.X, ALU.add))
            link(v.reciprocal(gB[:], gA[:]))
            link(v.tensor_tensor(lg[:, :, 0:E1], lg2[:, :, 0:E1], over(gB[:], E1), ALU.mult))
            top_mask(E1, TOP1)
            link(v.tensor_tensor(gat[:], gat[:], lg[:, :, 0:E1], ALU.mult))
            link(v.tensor_reduce(gA[:], gat[:], AX.X, ALU.add))
            link(v.tensor_scalar(gA[:], gA[:], EPS, None, ALU.add))
            link(v.reciprocal(gB[:], gA[:]))
            link(v.tensor_tensor(gat[:], gat[:], over(gB[:], E1), ALU.mult))
            link(v.tensor_reduce(gC[:], gat[:], AX.X, ALU.add))
            link(v.tensor_scalar(gA[:], gC[:], EPS, None, ALU.max))
            link(v.reciprocal(gB[:], gA[:]))
            link(v.tensor_tensor(gat[:], gat[:], over(gB[:], E1), ALU.mult))
            link(v.tensor_scalar(gC[:], gC[:], EPS, None, ALU.mult))
            for tb in range(TB):
                v.tensor_scalar(X[:, tb], X[:, tb], gC[:, tb:tb + 1], None, ALU.add).then_inc(s_m1, 2)
            with dve.Fori(0, E1 // 2) as ep:
                for tb, o in SUMS:
                    if o == 0:
                        dve.wait_ge(s_y1, ep * TB + tb + 1)
                        dve.wait_ge(s_m1, ep * (2 * TB) + 2 * TB)
                    else:
                        dve.wait_ge(s_m1, ep * (2 * TB) + 2 * TB + SUMS.index((tb, 0)) + 1)
                    v.scalar_tensor_tensor(X[:, tb], PS[tb % 8][:, o * D:o * D + D],
                                           gat_flat[:, bass.ds(2 * ep + tb * E1 + o, 1)], X[:, tb],
                                           ALU.mult, ALU.add).then_inc(s_m1, 1)


def kernel(**inputs):
    import numpy as np
    import concourse.bacc as bacc
    from concourse.bass_utils import run_bass_kernel_spmd

    x = {k: np.asarray(a) for k, a in inputs.items()}
    f = np.float32
    col = lambda a, n: a.reshape(n, P).T
    packed = np.concatenate([
        col(x["L0_xattn_bq"], 2), col(x["L0_xattn_bk"], 2), col(x["L0_ffn_ln1_w"], 2), col(x["L0_ffn_ln1_b"], 2),
        col(x["L0_ffn_ln2_w"], 2), col(x["L0_ffn_ln2_b"], 2), col(x["L0_ffn_bqkv"], 6),
        col(x["L1_xattn_bq"], HP), col(x["L1_xattn_bk"], HP)], axis=1)
    p = np.arange(P)
    masks = np.zeros((P, 8, P), f)
    for s in range(8):
        masks[:, s] = np.where(p[None, :] > IT * s + (p // HG)[:, None], f(-1e30), f(0))
    selm = np.zeros((P, HG, P), f)
    for h in range(HG):
        selm[:, h] = (p[:, None] // DH0 == h) & (p[:, None] % DH0 == p[None, :] % DH0)
    arrays = {
        "x": x["x"].reshape(T, D), "ctxT": x["ctx_1024"].reshape(T, D).T,
        "wq0T": x["L0_xattn_Wq"].T, "wk0T": x["L0_xattn_Wk"].T, "wv0T": x["L0_xattn_Wv"].T,
        "ErT": x["L0_xattn_Er"].T, "bv0": x["L0_xattn_bv"], "bvf": x["L0_ffn_bqkv"][2 * D:], "bof": x["L0_ffn_bo"],
        "cols": packed, "ident": np.eye(P, dtype=f),
        "hm4": np.where(p[:, None] // DH0 == np.arange(HG)[None, :], f(DH0 ** -0.5), f(0)),
        "hm8": np.where(p[:, None] // DH1 == np.arange(2)[None, :], f(DH1 ** -0.5), f(0)),
        "sel": selm, "maskc": masks,
        "wqkv": x["L0_ffn_Wqkv"], "wo": x["L0_ffn_Wo"], "gate_w": x["L0_ffn_gate_W"],
        "fc1T": x["L0_ffn_fc1_w"].transpose(0, 2, 1), "fc2T": x["L0_ffn_fc2_w"].transpose(0, 2, 1),
        "fc1b": x["L0_ffn_fc1_b"].reshape(E0, FK, P).transpose(0, 2, 1), "fc2b": x["L0_ffn_fc2_b"],
        "wq1": x["L1_xattn_Wq"].reshape(D, H1 * DH1), "wk1": x["L1_xattn_Wk"].reshape(D, H1 * DH1),
        "wv1": x["L1_xattn_Wv"].reshape(D, H1 * DH1), "wo1": x["L1_xattn_Wo"].reshape(H1 * DH1, D),
        "bv1": x["L1_xattn_bv"].reshape(-1), "bo1": x["L1_xattn_bo"],
        "rwT": x["L1_ffn_router_w"].T, "rb": x["L1_ffn_router_b"], "we": x["L1_ffn_expert_w"],
    }
    nc = bacc.Bacc("TRN2", target_bir_lowering=False, num_devices=1)
    given, A = {}, {}
    for name, a in arrays.items():
        a = np.ascontiguousarray(a)
        given[f"in_{name}"] = a
        A[name] = nc.dram_tensor(f"in_{name}", a.shape, mybir.dt.from_np(a.dtype), kind="ExternalInput").ap()
    out = nc.dram_tensor("out_0", (T, D), F32, kind="ExternalOutput").ap()
    build(nc, A, out)
    r = run_bass_kernel_spmd(nc, [given], core_ids=[0])
    return r.results[0]["out_0"].reshape(B, S, D)
```

```python
from contextlib import ExitStack

import concourse.bass as bass
from concourse import mybir

ALU = mybir.AluOpType
ACT = mybir.ActivationFunctionType
AX = mybir.AxisListType
F32 = mybir.dt.float32
F32R = mybir.dt.float32r
BF16 = mybir.dt.bfloat16
I32 = mybir.dt.int32

P = 128
D = 256
DK = D // P
B, S = 4, 512
T = B * S
TB = T // P
RT = S // P
H0, DH0 = 16, 16
HG = P // DH0
HH = H0 // HG
IT = P // HG
VW0 = DH0 + 1
ERW = S + 16
E0, F0 = 8, 1024
FK = F0 // P
H1, DH1 = 16, 64
HP = H1 // 2
IT1 = P // 2
VW1 = DH1 + 1
E1 = 16
TOP0, TOP1 = 2, 6
LN_EPS = 1e-5
EPS = 1e-10
LOW = -3e38

NT0 = TOP0 * T // P + E0
NTAB = TB + E0 * E0 + NT0 + E0

ORDER = (1, 2, 3, 0)
UNITS = [(r, t, RT // (r + 1)) for r in ORDER for t in range(0, 8, RT // (r + 1))]
NU = len(UNITS)
ALL_UNITS = [(hh, *u) for hh in range(HH) for u in UNITS]
NUA = len(ALL_UNITS)
GROUPS = [(hh, r) for hh in range(HH) for r in ORDER]
NG = len(GROUPS)
LAST_UNIT = [max(i for i, (hh, r, _, _) in enumerate(ALL_UNITS) if (hh, r) == g) for g in GROUPS]
PV_AT = [[] for _ in range(NUA + 3)]
for _g in range(NG):
    _first = LAST_UNIT[_g] + 3
    _n = max(LAST_UNIT[_g + 1] - LAST_UNIT[_g] - 1, 2) if _g + 1 < NG else 1
    for _h in range(HG):
        PV_AT[_first + _h * _n // HG].append((_g, _h))
PV_DONE = [max(n for n, at in enumerate(PV_AT) if (g, HG - 1) in at) for g in range(NG)]
Q_AT, SPREAD_AT, QLO_AT, SEL_AT = 0, (1, 3, 5, 7), 8, (9, 11, 12, 14, 15, 17, 18, 20)

COLS = {}
_at = 0
for _name, _n in [("bq0", 2), ("bk0", 2), ("ln1w", 2), ("ln1b", 2), ("ln2w", 2), ("ln2b", 2), ("bqkv", 6),
                  ("bq1", HP), ("bk1", HP)]:
    COLS[_name] = _at
    _at += _n
NCOLS = _at


def build(nc, A, out):
    with ExitStack() as ctx:
        sem = lambda name: ctx.enter_context(nc.semaphore(name))

        base = nc.sbuf_base + 31 & ~31
        at = [base]

        def region(nbytes):
            o = at[0]
            at[0] += nbytes + 31 & ~31
            assert at[0] <= nc.sbuf_usable_end, at[0]
            return o

        def place(name, shape, dt, o=None):
            n = 1
            for s in shape[1:]:
                n *= s
            nbytes = n * (2 if dt == BF16 else 4)
            return nc.alloc_sbuf_tensor_at(name, shape, dt, offset=region(nbytes) if o is None else o)

        KB = 1024
        X = place("X", [P, TB, D], F32)
        rQB = region(32 * KB)
        rKT = region(16 * KB)
        rR1 = region(32 * KB)
        NT = place("NT", [P, DK, T], F32)
        rVE = region(TB * H0 * VW0 * 4)
        rPT = region(28 * KB)
        Pb = place("Pb", [P, 4, S], F32)
        rW0 = region(6 * KB)
        rWF = region(8 * KB)
        rQS = region(8 * KB)
        nrm = place("nrm", [P, 4, D], F32)
        KT = place("KT", [P, HH, T], F32, rKT)
        VE = place("VE", [P, TB, H0, VW0], F32, rVE)
        RB = place("RB", [P, HH, S // 8, 8, HG], F32, rR1)
        CT0 = place("CT0", [P, DK, T], F32, rR1)
        Hs = place("Hs", [P, TB, D], F32, rR1)
        ON = place("ON", [P, TB, D], F32, rR1 + 16 * KB)
        QB = place("QB", [P, HH, S, HG], F32, rQB)
        PT = [place("PT0", [P, 3, 8, P], F32, rPT), place("PT1", [P, 4, 8, P], F32, rPT + 12 * KB)]
        ErS = place("ErS", [P, ERW], F32)
        W0 = place("W0", [P, 3, DK, D], F32, rW0)
        WF = place("WF", [P, DK, 3 * D], F32, rWF)
        WO = place("WO", [P, DK, D], F32, rWF + 6 * KB)
        qhi = place("qhi", [P, S], F32R, rQS)
        qlo = place("qlo", [P, S], F32R, rQS + 2 * KB)
        sel = place("sel", [P, HG, P], F32R, rQS + 4 * KB)
        sel_f = place("sel_f", [P, HG, P], F32, rQB)
        mask_f = place("mask_f", [P, 8, P], F32, rQB + 4 * KB)
        EW = place("EW", [P, E0, (DK * F0 + FK * D)], F32, rQB)
        assert rPT + 16 * KB >= rQB + E0 * 16 * KB
        NM = place("NM", [P, TB, D], F32, rPT + 16 * KB)
        zero = place("zero", [P, 8, D], F32, rWF)
        xin = [place(f"xin{i}", [P, D], F32, rW0 + KB * i) for i in range(2)]
        ysb = [place(f"ysb{i}", [P, D], F32, rW0 + 2 * KB + KB * i) for i in range(2)]
        xT = place("xT", [P, DK, P], F32, rW0 + 4 * KB)
        hS = place("hS", [P, F0], F32, rWF)
        hT = place("hT", [P, FK, P], F32, rWF + 4 * KB)
        B1 = place("B1", [P, FK, E0], F32)
        B1t = place("B1t", [P, NT0, FK], F32, rPT + 32 * KB)
        b1c = [place(f"b1c{i}", [P, FK], F32) for i in range(2)]
        rconst = place("rconst", [P, 2 * P], F32, rWF)
        rtab = place("rtab", [P, NTAB], F32, rWF + KB)
        pick = place("pick", [P, NT0, E0], F32, rWF + 2 * KB)
        prod = place("prod", [P, NT0, E0], F32, rWF + 4 * KB)
        msk = place("msk", [P, TB + 1, E0], F32, rPT + 34 * KB)
        rk = place("rk", [P, TB + 1, E0], F32, rPT + 35 * KB)
        small = [place(f"small{i}", [P, E0], F32) for i in range(4)]
        pos_f = [place(f"pos_f{i}", [P, TB], F32) for i in range(2)]
        pos = [place(f"pos{i}", [P, TB], I32) for i in range(2)]
        gpair = [place(f"gpair{i}", [P, TB], F32) for i in range(2)]
        te_f = place("te_f", [P, NT0], F32)
        te = place("te", [P, NT0], I32)
        YP = [place("YP0", [P, TB, D], F32, rQB + 16 * KB), place("YP1", [P, TB, D], F32, rPT)]
        W1 = place("W1", [P, 3, DK, H1 * DH1], F32, rR1)
        WO1 = place("WO1", [P, 8, D], F32, rR1 + 24 * KB)
        CTb = place("CTb", [P, DK, S], F32, rKT)
        K1hi = place("K1hi", [P, HP, S], F32R, rQB)
        K1lo = place("K1lo", [P, HP, S], F32R, rWF)
        O1 = place("O1", [P, RT, H1 * DH1], F32, rQB + 16 * KB)
        V1 = place("V1", [P, RT, H1, VW1], F32, rVE)
        QBhi = [place(f"QBhi{i}", [P, S, 2], F32R, rPT + 4 * KB * i) for i in range(2)]
        QBlo = [place(f"QBlo{i}", [P, S, 2], F32R, rKT + 8 * KB + 4 * KB * i) for i in range(2)]
        q1hi = place("q1hi", [P, S], F32R, rPT + 24 * KB)
        q1lo = place("q1lo", [P, S], F32R, rPT + 26 * KB)
        PT1 = [place(f"PTb{i}", [P, RT, 2 * P], F32, rPT + 8 * KB + 4 * KB * i) for i in range(2)]
        O1T = [place(f"O1T{i}", [P, 8, P], F32, rPT + 16 * KB + 4 * KB * i) for i in range(2)]
        rows1 = place("rows1", [P, H1 * DH1 + D], F32, rW0)
        WE = place("WE", [P, DK, E1, D], F32, rQB)
        NThi = place("NThi", [P, DK, T], F32R, rR1)
        NTlo = place("NTlo", [P, DK, T], F32R, rR1 + 16 * KB)
        WEhi = [place(f"WEhi{i}", [P, DK, 2 * D], F32R, rPT + 4 * KB * i) for i in range(2)]
        WElo = [place(f"WElo{i}", [P, DK, 2 * D], F32R, rPT + 8 * KB + 4 * KB * i) for i in range(2)]
        RW = place("RW", [P, DK, E1], F32)
        GW = place("GW", [P, DK, E0], F32)
        fc2b = place("fc2b", [E0, D], F32)
        rb_row = place("rb_row", [P, E1], F32)

        idf = place("idf", [P, P], F32)
        idb = place("idb", [P, P], BF16)
        maskb = place("maskb", [P, 8, P], BF16)
        hm4 = place("hm4", [P, HG], F32)
        hm8 = place("hm8", [P, 2], F32)
        cols = place("cols", [P, NCOLS], F32)
        rows0 = place("rows0", [P, 3, D], F32)
        st = place("st", [P, TB, 6], F32)
        mv = place("mv", [P, TB, 2], F32)
        sd = place("sd", [P, TB], F32)
        rstd = place("rstd", [P, TB], F32)
        nm = place("nm", [P, 16], F32)
        rec = place("rec", [P, 8], F32)
        tmp = place("tmp", [P, P], F32)
        eps_c = place("eps_c", [P, 1], F32)
        lg = place("lg", [P, TB, E1 + 8], F32)
        lg2 = place("lg2", [P, TB, E1 + 8], F32)
        top = place("top", [P, TB, 8], F32)
        gat = place("gat", [P, TB, E1], F32)
        gA = place("gA", [P, TB], F32)
        gB = place("gB", [P, TB], F32)
        gC = place("gC", [P, TB], F32)
        gT = place("gT", [E0, TB, P], F32, rQS)

        PS = [ctx.enter_context(nc.psum_tensor(f"PS{i}", [P, 512], F32)) for i in range(8)]
        SC, TR, OB, G = PS[0:3], PS[3:5], PS[5], PS[6:8]

        xs = nc.dram_tensor("pair_tokens", (NT0 * P, D), F32, kind="Internal").ap()
        ys = nc.dram_tensor("pair_outputs", (NT0 * P, D), F32, kind="Internal").ap()

        ld = {k: sem("ld_" + k) for k in
              ("ctx0", "w0", "const", "x", "er", "wf", "late", "route", "ew", "w1kv", "w1", "ctx1", "rows1", "we0", "we")}
        s_er0 = sem("s_er0")
        s_init = sem("s_init")
        s_eps = sem("s_eps")
        g_full = [sem(f"g_full{i}") for i in range(2)]
        g_free = [sem(f"g_free{i}") for i in range(2)]
        chain = sem("dve_chain")
        s_out = sem("s_out")

        KV1 = HP + 2 * RT
        PER1 = HP + KV1 + 3 * RT
        USE, N_USE = {}, {}
        n_use = 0
        for name, n in [("kv0", 24), ("ln0", TB), ("q0", B * 2 * (1 + HG)), ("ln1", TB), ("kvf", 24), ("qf", 2 * B),
                        ("ont", TB), ("wo", TB), ("ln2", TB), ("rt0", 1), ("rank", 1), ("gt", 4), ("kv1", KV1), ("ln3", TB),
                        ("p1", B * PER1 - KV1), ("ln4", TB), ("rt1", 1)]:
            USE[name], N_USE[name] = n_use, n
            n_use += n

        def slot(name, j, b=0, per=0):
            u = USE[name] + j
            return u % 2, u // 2 + b * (per // 2)

        def kv1_use(b):
            return ("kv1", 0, 0, 0) if isinstance(b, int) and b == 0 else ("p1", HP, b - 1, PER1)

        def wo1_at(final):
            return HP if final else HP + KV1

        def bank_for_write(eng, name, j, b=0, per=0):
            i, k = slot(name, j, b, per)
            eng.wait_ge(g_free[i], k)
            return G[i]

        def wrote(ins, name, j):
            ins.then_inc(g_full[slot(name, j)[0]], 1)

        def bank_for_read(eng, name, j, b=0, per=0):
            i, k = slot(name, j, b, per)
            eng.wait_ge(g_full[i], k + 1)
            return G[i]

        def has_read(ins, name, j):
            ins.then_inc(g_free[slot(name, j)[0]], 1)

        def wait_stored(eng, name, j, b=0, per=0):
            i, k = slot(name, j, b, per)
            eng.wait_ge(g_free[i], k + 1)

        def wait_all_stored(eng, name):
            u = USE[name] + N_USE[name]
            for i in range(2):
                eng.wait_ge(g_free[i], (u + 1 - i) // 2)

        def wait_all_written(eng, name, j, b=0, per=0):
            i, k = slot(name, j + KV1 - 1, b, per)
            eng.wait_ge(g_full[i], k + 1)

        ln_sem = {t: {k: sem(f"ln{t}_{k}") for k in ("var", "sd", "nrm")} for t in range(5)}
        ln_sem["h"] = {k: sem(f"lnh_{k}") for k in ("var", "sd", "nrm")}

        class AttnSems:
            def __init__(self, tag):
                self.sc = sem(tag + "_scores")
                self.nm = sem(tag + "_negmax")
                self.ex = sem(tag + "_exp")
                self.tr = sem(tag + "_transposed")
                self.pt = sem(tag + "_pt")
                self.pv = sem(tag + "_pv")
                self.rc = sem(tag + "_recip")
                self.mu = sem(tag + "_norm")
                self.o = sem(tag + "_out")
        at0, atf, at1 = AttnSems("a0"), AttnSems("af"), AttnSems("a1")
        s_qhi = sem("qhi")
        s_hb = sem("hs_plus_bias")
        s_xh = sem("x_plus_hs")
        s_xb = sem("x_plus_bo1")
        s_gate = sem("gates")
        s_e = {k: sem("moe0_" + k) for k in
               ("y", "x",
                "xt", "xT",
                "f", "hS",
                "tr", "hT",
                "yp", "ys",
                "b1",
                "idx", "te")}
        s_zero = sem("zero")
        s_xz = sem("pair_tokens_zeroed")
        s_xs = sem("pair_tokens")
        s_xin = [sem(f"moe0_xin{i}") for i in range(2)]
        s_yst = [sem(f"moe0_stored{i}") for i in range(2)]
        s_yp = [sem(f"pair_outputs{i}") for i in range(4)]
        s_rt = {k: sem("router_" + k) for k in ("mask", "in0", "exp0", "in1", "exp1")}
        s_y1 = sem("moe1_y")
        s_m1 = sem("moe1_acc")
        s_khi = sem("a1_keys_high")
        s_q1 = sem("a1_queries_split")
        s_lo = sem("moe1_tokens_split")
        s_wh = sem("moe1_weights_high")
        s_ws = sem("moe1_weights_split")
        SUMS = [(0, 0)]
        for tb in range(1, TB):
            SUMS += [(tb, 0), (tb - 1, 1)]
        SUMS += [(TB - 1, 1)]

        block = ctx.enter_context(nc.Block())

        @block.sync
        def _(sp):
            sp.dma_start(CT0[:], A["ctxT"].rearrange("(k p) t -> p k t", p=P)).then_inc(ld["ctx0"], 16)
            for i, w in enumerate(("wq0T", "wk0T", "wv0T")):
                sp.dma_start(W0[:, i], A[w].rearrange("(k p) n -> p k n", p=P)).then_inc(ld["w0"], 16)
            for dst, src in ((cols[:], A["cols"]), (idf[:], A["ident"]), (hm4[:], A["hm4"]), (hm8[:], A["hm8"]),
                             (sel_f[:], A["sel"]), (mask_f[:], A["maskc"])):
                sp.dma_start(dst, src).then_inc(ld["const"], 16)
            for i, r in enumerate(("bv0", "bvf", "bof")):
                sp.dma_start(rows0[:, i], A[r].partition_broadcast(P)).then_inc(ld["const"], 16)
            sp.dma_start(X[:], A["x"].rearrange("(t p) d -> p t d", p=P)).then_inc(ld["x"], 16)
            sp.wait_ge(s_er0, 1)
            for g in range(HG):
                sp.dma_start(ErS[DH0 * g:DH0 * g + DH0, g:g + S], A["ErT"]).then_inc(ld["er"], 16)
            sp.wait_ge(s_zero, 1)
            for i in range(NT0 // 8):
                sp.dma_start(xs.rearrange("(t p) d -> p t d", p=P)[:, 8 * i:8 * i + 8], zero[:]).then_inc(s_xz, 16)
            sp.wait_ge(s_xz, 16 * (NT0 // 8))
            sp.dma_start(WF[:], A["wqkv"].rearrange("(k p) n -> p k n", p=P)).then_inc(ld["wf"], 16)
            sp.dma_start(WO[:], A["wo"].rearrange("(k p) n -> p k n", p=P)).then_inc(ld["wf"], 16)
            sp.dma_start(GW[:], A["gate_w"].rearrange("(k p) n -> p k n", p=P)).then_inc(ld["late"], 16)
            sp.dma_start(RW[:], A["rwT"].rearrange("(k p) n -> p k n", p=P)).then_inc(ld["late"], 16)
            sp.dma_start(fc2b[:], A["fc2b"]).then_inc(ld["late"], 16)
            sp.dma_start(rb_row[:], A["rb"].partition_broadcast(P)).then_inc(ld["late"], 16)
            sp.dma_start(B1[:], A["fc1b"]).then_inc(ld["late"], 16)

            def expert_weights(e):
                sp.dma_start(EW[:, e, 0:DK * F0].rearrange("p (k f) -> p k f", k=DK),
                             A["fc1T"][e].rearrange("(k p) f -> p k f", p=P)).then_inc(ld["ew"], 16)
                sp.dma_start(EW[:, e, DK * F0:].rearrange("p (k d) -> p k d", k=FK),
                             A["fc2T"][e].rearrange("(k p) d -> p k d", p=P)).then_inc(ld["ew"], 16)

            sp.wait_ge(atf.sc, B * NUA)
            for e in (0, 1, 2):
                expert_weights(e)
            sp.wait_ge(atf.pv, B * NG)
            for e in (6, 7):
                expert_weights(e)
            wait_all_stored(sp, "ont")
            expert_weights(4)
            wait_all_stored(sp, "wo")
            sp.dma_start(rconst[:], A["rconst"]).then_inc(ld["route"], 16)
            sp.dma_start(rtab[:], A["rtab"]).then_inc(ld["route"], 16)
            sp.wait_ge(s_xh, TB)
            sp.wait_ge(ln_sem[2]["nrm"], TB)
            expert_weights(3)
            wait_stored(sp, "rt0", 0)
            expert_weights(5)

            def load_tokens(j, s):
                sp.dma_start(xin[s][:], xs[bass.ds(j * P, P), :]).then_inc(s_xin[s], 16)

            def store_outputs(j, s):
                sp.wait_ge(s_e["ys"], j + 1)
                sp.dma_start(ys[bass.ds(j * P, P), :], ysb[s][:]).then_inc(s_yst[s], 16)

            def moe0_tile(j, s, first=False, last=False):
                if not last:
                    sp.wait_ge(s_e["xt"], j + 1)
                    load_tokens(j + 2, s)
                if not first:
                    store_outputs(j - 1, 1 - s)

            sp.wait_ge(s_xs, 16 * TOP0 * TB)
            load_tokens(0, 0)
            load_tokens(1, 1)
            moe0_tile(0, 0, first=True)
            moe0_tile(1, 1)
            with sp.Fori(1, NT0 // 2 - 1) as jp:
                for s in range(2):
                    moe0_tile(2 * jp + s, s)
            moe0_tile(NT0 - 2, 0, last=True)
            moe0_tile(NT0 - 1, 1, last=True)
            store_outputs(NT0 - 1, 1)

            def context(b):
                sp.dma_start(CTb[:], A["ctxT"].rearrange("(k p) t -> p k t", p=P)[:, :, bass.ds(b * S, S)])\
                    .then_inc(ld["ctx1"], 16)

            context(0)
            for i, w, name in ((1, "wk1", "w1kv"), (2, "wv1", "w1kv"), (0, "wq1", "w1")):
                sp.dma_start(W1[:, i], A[w].rearrange("(k p) n -> p k n", p=P)).then_inc(ld[name], 16)
            sp.wait_ge(s_yst[0], 16 * (NT0 // 2))
            sp.wait_ge(s_yst[1], 16 * (NT0 // 2))
            sp.dma_start(rows1[:, 0:H1 * DH1], A["bv1"].partition_broadcast(P)).then_inc(ld["rows1"], 16)
            sp.dma_start(rows1[:, H1 * DH1:], A["bo1"].partition_broadcast(P)).then_inc(ld["rows1"], 16)
            sp.dma_start(WO1[:], A["wo1"].rearrange("(k p) n -> p k n", p=P)).then_inc(ld["w1"], 16)
            wait_all_written(sp, "kv1", 0)
            context(1)
            with sp.Fori(1, B - 1) as b:
                wait_all_written(sp, "p1", HP, b - 1, PER1)
                context(b + 1)
            i, k = slot("p1", B * PER1 - KV1 - 1)
            sp.wait_ge(g_full[i], k + 1)
            for name, e0, e1 in (("we0", 0, 2), ("we", 2, E1)):
                for k in range(DK):
                    sp.dma_start(WE[:, k, e0:e1], A["we"][e0:e1, k * P:k * P + P, :].rearrange("e p n -> p e n"))\
                        .then_inc(ld[name], 16)
            sp.wait_ge(s_m1, TB * E1 + 2 * TB)
            for i in range(4):
                sp.dma_start(out.rearrange("(t p) d -> p t d", p=P)[:, 4 * i:4 * i + 4], X[:, 4 * i:4 * i + 4])\
                    .then_inc(s_out, 16)
            sp.wait_ge(s_out, 64)

        @block.gpsimd
        def _(pool):
            nc.gpsimd.memset(ErS[:], 0.0).then_inc(s_er0, 1)
            nc.gpsimd.memset(eps_c[:], LN_EPS).then_inc(s_eps, 1)
            nc.gpsimd.memset(zero[:], 0.0).then_inc(s_zero, 1)
            pool.wait_ge(ld["const"], 16 * 9)
            for tb in range(TB):
                pool.wait_ge(ln_sem[1]["nrm"], tb + 1)
                nc.gpsimd.tensor_tensor(Hs[:, tb], Hs[:, tb], rows0[:, 2], ALU.add).then_inc(s_hb, 1)
            for tb in range(TB):
                wait_stored(pool, "wo", tb)
                nc.gpsimd.tensor_tensor(X[:, tb], X[:, tb], Hs[:, tb], ALU.add).then_inc(s_xh, 1)
            pool.wait_ge(s_xz, 16 * (NT0 // 8))
            pool.wait_ge(s_e["idx"], 2)
            for tb in range(TB):
                for i in range(TOP0):
                    pool.indirect_dma_start(xs, bass.IndirectOffsetOnAxis(pos[i][:, tb:tb + 1], 0), NM[:, tb, :],
                                            None).then_inc(s_xs, 16)
            for s in range(2):
                pool.wait_ge(s_yst[s], 16 * (NT0 // 2))
            for tb in range(TB):
                for i in range(TOP0):
                    pool.indirect_dma_start(YP[i][:, tb, :], None, ys,
                                            bass.IndirectOffsetOnAxis(pos[i][:, tb:tb + 1], 0))\
                        .then_inc(s_yp[tb // 4], 16)
            pool.wait_ge(ld["rows1"], 32)
            for tb in range(TB):
                pool.wait_ge(ln_sem[3]["nrm"], tb + 1)
                nc.gpsimd.tensor_tensor(X[:, tb], X[:, tb], rows1[:, H1 * DH1:], ALU.add).then_inc(s_xb, 1)
            for tb in range(TB):
                wait_stored(pool, "ln4", tb)
                t = slice(tb * P, tb * P + P)
                nc.gpsimd.tensor_tensor(NTlo[:, :, t], NT[:, :, t], NThi[:].bitcast(F32)[:, :, t], ALU.subtract)\
                    .then_inc(s_lo, 1)

        @block.tensor
        def _(pe):
            mm = nc.tensor.matmul

            def project(bank, w, src, n, m=P):
                for k in range(DK):
                    last = mm(bank[0:m, 0:n], w(k), src(k), start=(k == 0), stop=(k == DK - 1))
                return last

            def keys_values(name, wk, wv, src_k, src_v):
                for hh in range(HH):
                    for b in range(B):
                        j = hh * B + b
                        bank = bank_for_write(pe, name, j)
                        wrote(project(bank, lambda k: wk(k, hh), lambda k: src_k(k, b), S), name, j)
                for tb in range(TB):
                    j = 8 + tb
                    bank = bank_for_write(pe, name, j)
                    wrote(project(bank, lambda k: src_v(k, tb), wv, D), name, j)

            def ln_transposes(t, name, src):
                for tb in range(TB):
                    bank = bank_for_write(pe, name, tb)
                    pe.wait_ge(ln_sem[t]["nrm"], tb + 1)
                    for k in range(DK):
                        last = nc.tensor.transpose(bank[:, k * P:k * P + P], src(tb)[:, k * P:k * P + P], idf[:])
                    wrote(last, name, tb)

            def queries0(name, hh, b, w):
                per, j = HH * (1 + HG if name == "q0" else 1), hh * (1 + HG if name == "q0" else 1)
                bank = bank_for_write(pe, name, j, b, per)
                wrote(project(bank, lambda k: w(k, hh), lambda k: NT[:, k, bass.ds(b * S, S)], S), name, j)

            def repeat0(hh, b, h):
                per, j = HH * (1 + HG), hh * (1 + HG) + 1 + h
                if h == 0:
                    pe.wait_ge(s_qhi, b * HH + hh + 1)
                    wait_stored(pe, "q0", j - 1, b, per)
                bank = bank_for_write(pe, "q0", j, b, per)
                mm(bank[:], sel[:, h], qhi[:], start=True, stop=False)
                wrote(mm(bank[:], sel[:, h], qlo[:], start=False, stop=True), "q0", j)

            def prepare0(rel, b, n, last):
                hh, n = divmod(n, NU)
                if last and hh == HH - 1:
                    return
                nb, nh = (b, 1) if hh == 0 else (b + 1, 0)
                if n == Q_AT:
                    queries0("q0" if rel else "qf", nh, nb, WQ0 if rel else WQF)
                if rel and n in SEL_AT:
                    repeat0(nh, nb, SEL_AT.index(n))

            def attention0(a, b, rel, last):
                def scores(n):
                    hh, r, t0, tiles = ALL_UNITS[n]
                    if n % NU == 0:
                        if rel:
                            wait_stored(pe, "q0", hh * (1 + HG) + HG, b, HH * (1 + HG))
                            wait_stored(pe, "q0", hh * (1 + HG) + HG - 1, b, HH * (1 + HG))
                        else:
                            wait_stored(pe, "qf", hh, b, HH)
                    if n >= 3:
                        pe.wait_ge(a.ex, b * NUA + n - 2)
                    for i in range(tiles):
                        t = 8 * r + t0 + i
                        o, w = i * P * (r + 1), IT * (t + 1)
                        mm(SC[n % 3][:, o + r * P:o + r * P + P], idb[:], maskb[:, t % 8, :], start=True, stop=False,
                           skip_group_check=True)
                        ins = mm(SC[n % 3][:, o:o + w], QB[:, hh, t * IT:t * IT + IT, :].rearrange("p i h -> p (i h)"),
                                 KT[:, hh, bass.ds(b * S, w)], start=False, stop=not rel, skip_group_check=True)
                        for u in range(2 if rel else 0):
                            e = S - 1 - IT * t - 8 * u
                            ins = mm(SC[n % 3][64 * u:64 * u + 64, o:o + w],
                                     RB[:, hh, 2 * t + u].rearrange("p i h -> p (i h)"),
                                     ErS[:, e:e + w], start=False, stop=(u == 1), skip_group_check=True)
                    ins.then_inc(a.sc, 1)

                def transposes(n):
                    _, r, _, tiles = ALL_UNITS[n]
                    pe.wait_ge(a.ex, b * NUA + n + 1)
                    if n >= 2:
                        pe.wait_ge(a.pt, b * NUA + n - 1)
                    for c in range(r + 1):
                        for i in range(tiles):
                            o = i * P * (r + 1) + c * P
                            ins = nc.tensor.transpose(TR[n % 2][:, (c * tiles + i) * P:(c * tiles + i + 1) * P],
                                                      Pb[:, n % 4, o:o + P], idf[:])
                    ins.then_inc(a.tr, 1)

                def values(g, h):
                    hh, r = GROUPS[g]
                    if h == 0:
                        pe.wait_ge(a.pt, b * NUA + LAST_UNIT[g] + 1)
                        if g:
                            pe.wait_ge(a.mu, b * NG + g)
                    for c in range(r + 1):
                        lhsT = PT[r % 2][:, c].rearrange("p s (i h) -> p (s i) h", h=HG)[:, :, h]
                        rhs = VE[:, bass.ds(b * RT + c, 1), hh * HG + h, :]
                        ins = mm(OB[:, h * VW0:h * VW0 + VW0], lhsT, rhs,
                                 start=(c == 0), stop=(c == r), skip_group_check=True)
                    if h == HG - 1:
                        ins.then_inc(a.pv, 1)

                for n in range(NUA + 3):
                    if n < NUA:
                        prepare0(rel, b, n, last)
                        scores(n)
                    if 2 <= n < NUA + 2:
                        transposes(n - 2)
                    for g, h in PV_AT[n]:
                        values(g, h)

            WQ0 = lambda k, hh: W0[:, 0, k, hh * P:hh * P + P]
            WQF = lambda k, hh: WF[:, k, hh * P:hh * P + P]

            pe.wait_ge(ld["ctx0"], 16)
            pe.wait_ge(ld["w0"], 48)
            keys_values("kv0", lambda k, hh: W0[:, 1, k, hh * P:hh * P + P], lambda k: W0[:, 2, k, :],
                        lambda k, b: CT0[:, k, b * S:b * S + S], lambda k, tb: CT0[:, k, tb * P:tb * P + P])
            pe.wait_ge(ld["const"], 16 * 9)
            ln_transposes(0, "ln0", lambda tb: nrm[:, tb % 4])
            pe.wait_ge(ld["er"], 16 * HG)
            pe.wait_ge(s_init, 5)
            queries0("q0", 0, 0, WQ0)
            for h in range(HG):
                repeat0(0, 0, h)
            with pe.Fori(0, B - 1) as b:
                attention0(at0, b, True, False)
            attention0(at0, B - 1, True, True)

            ln_transposes(1, "ln1", lambda tb: nrm[:, tb % 4])
            pe.wait_ge(ld["wf"], 32)
            wait_all_stored(pe, "ln1")
            keys_values("kvf", lambda k, hh: WF[:, k, D + hh * P:D + hh * P + P], lambda k: WF[:, k, 2 * D:3 * D],
                        lambda k, b: NT[:, k, b * S:b * S + S], lambda k, tb: NT[:, k, tb * P:tb * P + P])
            queries0("qf", 0, 0, WQF)
            with pe.Fori(0, B - 1) as b:
                attention0(atf, b, False, False)
            attention0(atf, B - 1, False, True)
            for tb in range(TB):
                bank = bank_for_write(pe, "ont", tb)
                pe.wait_ge(atf.mu, NG * (tb // RT) + RT + ORDER.index(tb % RT) + 1)
                for k in range(DK):
                    last = nc.tensor.transpose(bank[:, k * P:k * P + P], ON[:, tb, k * P:k * P + P], idf[:])
                wrote(last, "ont", tb)
            for tb in range(TB):
                bank = bank_for_write(pe, "wo", tb)
                wait_stored(pe, "ont", tb)
                wrote(project(bank, lambda k: NT[:, k, tb * P:tb * P + P], lambda k: WO[:, k, :], D), "wo", tb)
            ln_transposes(2, "ln2", lambda tb: NM[:, tb])

            pe.wait_ge(ld["late"], 80)
            wait_all_stored(pe, "ln2")
            bank = bank_for_write(pe, "rt0", 0)
            for tb in range(TB):
                for k in range(DK):
                    last = mm(bank[:, tb * E0:tb * E0 + E0], NT[:, k, tb * P:tb * P + P], GW[:, k, :],
                              start=(k == 0), stop=(k == DK - 1), skip_group_check=True)
            wrote(last, "rt0", 0)
            pe.wait_ge(ld["route"], 32)
            pe.wait_ge(s_rt["mask"], 1)
            bank = bank_for_write(pe, "rank", 0)
            mm(bank[:, 0:(TB + 1) * E0], rconst[:, 0:P], msk[:].rearrange("p t e -> p (t e)"), start=True, stop=False,
               skip_group_check=True)
            for tb in range(TB):
                last = mm(bank[:, (tb + 1) * E0:(TB + 1) * E0].rearrange("p (t e) -> p t e", e=E0),
                          rconst[:, P:], msk[:, tb:tb + 1, :].to_broadcast([P, TB - tb, E0]),
                          start=False, stop=(tb == TB - 1), skip_group_check=True)
            wrote(last, "rank", 0)
            pe.wait_ge(s_gate, 1)
            for i in range(4):
                bank = bank_for_write(pe, "gt", i)
                for q in range(4):
                    last = nc.tensor.transpose(bank[0:E0, q * P:q * P + P], gat[:, i * 4 + q, 0:E0], idf[:])
                wrote(last, "gt", i)
            wait_all_stored(pe, "gt")
            for tb in range(TB):
                if tb >= 4:
                    pe.wait_ge(s_e["x"], tb - 3)
                mm(PS[2 + tb % 4][:, 0:D], gT[:, tb, :], fc2b[:], start=True, stop=True).then_inc(s_e["y"], 1)

            def tokens(s, count):
                pe.wait_ge(s_xin[s], count)
                for k in range(DK):
                    last = nc.tensor.transpose(PS[0][:, k * P:k * P + P], xin[s][:, k * P:k * P + P], idf[:])
                last.then_inc(s_e["xt"], 1)

            def expert_of(j):
                return pe.value_load(te[0:1, bass.ds(j, 1)])

            def down(j, e):
                pe.wait_ge(s_e["hT"], j + 1)
                for f in range(FK):
                    o = DK * F0 + f * D
                    last = mm(PS[5][:, 0:D], hT[:, f, :], EW[:, bass.ds(e, 1), o:o + D].rearrange("p e d -> p (e d)"),
                              start=(f == 0), stop=(f == FK - 1))
                last.then_inc(s_e["yp"], 1)

            def moe0_tile(j, s, xin_count, first=False, last=False):
                e = expert_of(j)
                e_last = None if first else expert_of(j - 1)
                pe.wait_ge(s_e["xT"], j + 1)
                for hf in range(2):
                    for k in range(DK):
                        o = k * F0 + hf * 512
                        ins = mm(PS[1 + hf][:], xT[:, k, :],
                                 EW[:, bass.ds(e, 1), o:o + 512].rearrange("p e f -> p (e f)"),
                                 start=(k == 0), stop=(k == DK - 1))
                    ins.then_inc(s_e["f"], 1)
                if not last:
                    tokens(1 - s, xin_count)
                if not first:
                    if not isinstance(j, int) or j >= 2:
                        pe.wait_ge(s_e["ys"], j - 1)
                    down(j - 1, e_last)
                for hf in range(2):
                    pe.wait_ge(s_e["hS"], 2 * j + 1 + hf)
                    for q in range(4):
                        f = hf * 4 + q
                        ins = nc.tensor.transpose(PS[3 + hf][:, q * P:q * P + P], hS[:, f * P:f * P + P], idf[:])
                    ins.then_inc(s_e["tr"], 1)

            pe.wait_ge(s_e["x"], TB)
            pe.wait_ge(s_e["te"], 1)
            pe.wait_ge(ld["ew"], 32 * E0)
            tokens(0, 16)
            moe0_tile(0, 0, 16, first=True)
            moe0_tile(1, 1, 32)
            with pe.Fori(1, NT0 // 2 - 1) as jp:
                for s in range(2):
                    moe0_tile(2 * jp + s, s, 16 * jp + 16 + 16 * s)
            moe0_tile(NT0 - 2, 0, 16 * (NT0 // 2))
            moe0_tile(NT0 - 1, 1, 0, last=True)
            e_last = expert_of(NT0 - 1)
            pe.wait_ge(s_e["ys"], NT0 - 1)
            down(NT0 - 1, e_last)

            def keys_values1(b):
                name, at, turn, per = kv1_use(b)
                pe.wait_ge(ld["ctx1"], b * 16 + 16)
                for m in range(HP):
                    bank = bank_for_write(pe, name, at + m, turn, per)
                    wrote(project(bank, lambda k: W1[:, 1, k, m * P:m * P + P],
                                  lambda k: CTb[:, k, :], S), name, at + m)
                for r in range(RT):
                    for hf in range(2):
                        j = at + HP + 2 * r + hf
                        bank = bank_for_write(pe, name, j, turn, per)
                        wrote(project(bank, lambda k: CTb[:, k, r * P:r * P + P],
                                      lambda k: W1[:, 2, k, hf * S:hf * S + S], S), name, j)

            pe.wait_ge(ld["w1kv"], 32)
            keys_values1(0)
            ln_transposes(3, "ln3", lambda tb: nrm[:, tb % 4])
            wait_all_stored(pe, "ln3")
            pe.wait_ge(ld["w1"], 32)

            def attention1(b, final=False):
                def queries(p):
                    bank = bank_for_write(pe, "p1", p, b, PER1)
                    wrote(project(bank, lambda k: W1[:, 0, k, p * P:p * P + P],
                                  lambda k: NT[:, k, bass.ds(b * S, S)], S), "p1", p)

                def scores(n):
                    p, it = divmod(n, 8)
                    if it == 0:
                        wait_stored(pe, "p1", p, b, PER1)
                    if n >= 3:
                        pe.wait_ge(at1.ex, b * 64 + n - 2)
                    for k, (q, keys) in enumerate(((QBhi, K1hi), (QBhi, K1lo), (QBlo, K1hi))):
                        ins = mm(SC[n % 3][:], q[p % 2][:, it * IT1:it * IT1 + IT1, :].rearrange("p i h -> p (i h)"),
                                 keys[:, p, :], start=(k == 0), stop=(k == 2))
                    ins.then_inc(at1.sc, 1)

                def transposes(n):
                    pe.wait_ge(at1.ex, b * 64 + n + 1)
                    if n >= 2:
                        pe.wait_ge(at1.pt, b * 64 + n - 1)
                    for c in range(RT):
                        last = nc.tensor.transpose(TR[n % 2][:, c * P:c * P + P], Pb[:, n % 4, c * P:c * P + P],
                                                   idf[:])
                    last.then_inc(at1.tr, 1)

                def values(g):
                    p, r = divmod(g, 4)
                    pe.wait_ge(at1.pt, b * 64 + 2 * g + 2)
                    if g:
                        pe.wait_ge(at1.mu, b * 32 + g)
                    for h in range(2):
                        for c in range(RT):
                            lhsT = PT1[g % 2][:, c].rearrange("p (i h) -> p i h", h=2)[:, :, h]
                            last = mm(OB[:, h * VW1:h * VW1 + VW1], lhsT, V1[:, c, 2 * p + h, :],
                                      start=(c == 0), stop=(c == RT - 1), skip_group_check=True)
                    last.then_inc(at1.pv, 1)

                for i in range(2):
                    if isinstance(b, int) and not b:
                        wait_stored(pe, "kv1", KV1 - 1 - i)
                    else:
                        wait_stored(pe, "p1", HP + KV1 - 1 - i, b - 1, PER1)
                queries(0)
                for n in range(64 + 4):
                    if n < 64:
                        if n % 8 == 1 and n < 56:
                            queries(n // 8 + 1)
                        scores(n)
                    if 2 <= n < 66:
                        transposes(n - 2)
                    if n >= 5 and (n - 5) % 2 == 0:
                        values((n - 5) // 2)
                if not final:
                    keys_values1(b + 1)
                for r in range(RT):
                    pe.wait_ge(at1.mu, b * 32 + 29 + r)
                    for hf in range(2):
                        j = wo1_at(final) + 3 * r + hf
                        bank = bank_for_write(pe, "p1", j, b, PER1)
                        for k in range(4):
                            kk = hf * 4 + k
                            last = nc.tensor.transpose(bank[:, k * P:k * P + P], O1[:, r, kk * P:kk * P + P], idf[:])
                        wrote(last, "p1", j)
                    j = wo1_at(final) + 3 * r + 2
                    bank = bank_for_write(pe, "p1", j, b, PER1)
                    wait_stored(pe, "p1", j - 2, b, PER1)
                    wait_stored(pe, "p1", j - 1, b, PER1)
                    for k in range(8):
                        last = mm(bank[:, 0:D], O1T[r % 2][:, k, :], WO1[:, k, :], start=(k == 0), stop=(k == 7))
                    wrote(last, "p1", j)

            attention1(0)
            with pe.Fori(1, B - 1) as b:
                attention1(b)
            attention1(B - 1, final=True)

            ln_transposes(4, "ln4", lambda tb: nrm[:, tb % 4])
            wait_all_stored(pe, "ln4")
            bank = bank_for_write(pe, "rt1", 0)
            for tb in range(TB):
                for k in range(DK):
                    last = mm(bank[:, tb * E1:tb * E1 + E1], NT[:, k, tb * P:tb * P + P], RW[:, k, :],
                              start=(k == 0), stop=(k == DK - 1), skip_group_check=True)
            wrote(last, "rt1", 0)
            with pe.Fori(0, E1 // 4) as eq:
                for i in range(2):
                    pe.wait_ge(s_ws, eq * 2 + i + 1)
                    for tb in range(TB):
                        read = SUMS.index(((tb - 8) % TB, 1)) + 1 + (0 if tb < 8 else 2 * TB)
                        pe.wait_ge(s_m1, eq * (4 * TB) + i * (2 * TB) + read)
                        pe.wait_ge(s_lo, tb + 1)
                        t = slice(tb * P, tb * P + P)
                        parts = [(NThi, WEhi), (NThi, WElo), (NTlo, WEhi)]
                        for n, (x, w) in enumerate(parts):
                            for k in range(DK):
                                last = mm(PS[tb % 8][:], x[:, k, t], w[i][:, k, :], start=(n + k == 0),
                                          stop=(n + k == len(parts) + DK - 2))
                        last.then_inc(s_y1, 1)

        @block.scalar
        def _(act):
            af = nc.scalar.activation

            def ln_part(t, name, w=None, bcol=None, transposed=True, split=False):
                act.wait_ge(ln_sem[t]["var"], 1)
                af(sd[:], mv[:, :, 1], ACT.Sqrt, bias=eps_c[:, 0:1]).then_inc(ln_sem[t]["sd"], 1)
                for tb in range(TB if transposed else 0):
                    bank = bank_for_read(act, name, tb)
                    if split:
                        af(NThi[:, :, tb * P:tb * P + P], bank[:, 0:D].rearrange("p (k q) -> p k q", k=DK), ACT.Copy)
                    for k in range(DK):
                        if w is None:
                            last = af(NT[:, k, tb * P:tb * P + P], bank[:, k * P:k * P + P], ACT.Identity)
                        else:
                            last = af(NT[:, k, tb * P:tb * P + P], bank[:, k * P:k * P + P], ACT.Identity,
                                      scale=cols[:, w + k:w + k + 1], bias=cols[:, bcol + k:bcol + k + 1])
                    has_read(last, name, tb)

            def keys(name, bcol):
                for hh in range(HH):
                    for b in range(B):
                        bank = bank_for_read(act, name, hh * B + b)
                        ins = af(KT[:, hh, b * S:b * S + S], bank[:], ACT.Identity,
                                 bias=cols[:, bcol + hh:bcol + hh + 1])
                        has_read(ins, name, hh * B + b)

            def high_parts(hh, b):
                per, j = HH * (1 + HG), hh * (1 + HG)
                bank = bank_for_read(act, "q0", j, b, per)
                wait_stored(act, "q0", j - 1, b, per)
                af(qhi[:], bank[:], ACT.Identity, bias=cols[:, COLS["bq0"] + hh:COLS["bq0"] + hh + 1])\
                    .then_inc(s_qhi, 1)

            def attention0(a, b, rel, last):
                for n in range(NUA + 2):
                    if n < NUA:
                        _, r, _, tiles = ALL_UNITS[n]
                        if rel and n == Q_AT:
                            high_parts(1, b)
                        if rel and n == NU + Q_AT and not last:
                            high_parts(0, b + 1)
                        act.wait_ge(a.nm, b * NUA + n + 1)
                        if n >= 4:
                            act.wait_ge(a.tr, b * NUA + n - 3)
                        w = P * (r + 1)
                        for i in range(tiles):
                            c = n % 4 * 4 + i
                            ins = af(Pb[:, n % 4, i * w:i * w + w], SC[n % 3][:, i * w:i * w + w], ACT.Exp,
                                     bias=nm[:, c:c + 1])
                        ins.then_inc(a.ex, 1)
                    if n >= 2:
                        m = n - 2
                        hh, r, t0, tiles = ALL_UNITS[m]
                        g = GROUPS.index((hh, r))
                        act.wait_ge(a.tr, b * NUA + m + 1)
                        if t0 == 0 and g >= 2:
                            act.wait_ge(a.pv, b * NG + g - 1)
                        af(PT[r % 2][:, 0:r + 1, t0:t0 + tiles, :].rearrange("p c t q -> p c (t q)"),
                           TR[m % 2][:, 0:(r + 1) * tiles * P].rearrange("p (c q) -> p c q", c=r + 1),
                           ACT.Copy).then_inc(a.pt, 1)

            act.wait_ge(ld["const"], 16 * 9)
            keys("kv0", COLS["bk0"])
            act.wait_ge(s_eps, 1)
            ln_part(0, "ln0")
            high_parts(0, 0)
            with act.Fori(0, B - 1) as b:
                attention0(at0, b, True, False)
            attention0(at0, B - 1, True, True)
            ln_part("h", None, transposed=False)
            ln_part(1, "ln1", COLS["ln1w"], COLS["ln1b"])
            keys("kvf", COLS["bqkv"] + 2)
            with act.Fori(0, B - 1) as b:
                attention0(atf, b, False, False)
            attention0(atf, B - 1, False, True)
            for tb in range(TB):
                bank = bank_for_read(act, "ont", tb)
                has_read(af(NT[:, :, tb * P:tb * P + P], bank[:, 0:D].rearrange("p (k q) -> p k q", k=DK),
                            ACT.Copy), "ont", tb)
            ln_part(2, "ln2", COLS["ln2w"], COLS["ln2b"])
            act.wait_ge(s_rt["in0"], 1)
            af(lg2[:, :, 0:E0], lg2[:, :, 0:E0], ACT.Exp).then_inc(s_rt["exp0"], 1)
            for i in range(4):
                bank = bank_for_read(act, "gt", i)
                has_read(af(gT[:, i * 4:i * 4 + 4, :], bank[0:E0, :].rearrange("p (q c) -> p q c", q=4), ACT.Copy),
                         "gt", i)
            def tokens(j):
                act.wait_ge(s_e["xt"], j + 1)
                for k in range(DK):
                    w, bcol = COLS["ln2w"] + k, COLS["ln2b"] + k
                    last = af(xT[:, k, :], PS[0][:, k * P:k * P + P], ACT.Identity, scale=cols[:, w:w + 1],
                              bias=cols[:, bcol:bcol + 1])
                last.then_inc(s_e["xT"], 1)

            def moe0_tile(j, s, last=False):
                if not last:
                    tokens(j + 1)
                act.wait_ge(s_e["b1"], j + 1)
                for f in range(FK):
                    if f % 4 == 0:
                        act.wait_ge(s_e["tr"], 2 * j + 1 + f // 4)
                    ins = af(hT[:, f, :], PS[3 + f // 4][:, f % 4 * P:f % 4 * P + P], ACT.Gelu,
                             bias=b1c[s][:, f:f + 1])
                ins.then_inc(s_e["hT"], 1)

            tokens(0)
            moe0_tile(0, 0)
            moe0_tile(1, 1)
            with act.Fori(1, NT0 // 2 - 1) as jp:
                for s in range(2):
                    moe0_tile(2 * jp + s, s)
            moe0_tile(NT0 - 2, 0)
            moe0_tile(NT0 - 1, 1, last=True)
            def keys1(b):
                name, at, turn, per = kv1_use(b)
                for m in range(HP):
                    bank = bank_for_read(act, name, at + m, turn, per)
                    af(K1hi[:, m, :], bank[:], ACT.Identity,
                       bias=cols[:, COLS["bk1"] + m:COLS["bk1"] + m + 1]).then_inc(s_khi, 1)

            keys1(0)
            ln_part(3, "ln3")

            def attention1(b, final=False):
                for n in range(64 + 2):
                    if n < 64:
                        act.wait_ge(at1.nm, b * 64 + n + 1)
                        if n >= 4:
                            act.wait_ge(at1.tr, b * 64 + n - 3)
                        af(Pb[:, n % 4, :], SC[n % 3][:], ACT.Exp, bias=nm[:, n % 4 * 4:n % 4 * 4 + 1])\
                            .then_inc(at1.ex, 1)
                    if n >= 2:
                        m = n - 2
                        g = m // 2
                        act.wait_ge(at1.tr, b * 64 + m + 1)
                        if m % 2 == 0 and g >= 2:
                            act.wait_ge(at1.pv, b * 32 + g - 1)
                        af(PT1[g % 2][:, :, (m % 2) * P:(m % 2) * P + P], TR[m % 2][:].rearrange("p (c q) -> p c q", c=RT),
                           ACT.Copy).then_inc(at1.pt, 1)
                if not final:
                    keys1(b + 1)
                for r in range(RT):
                    for hf in range(2):
                        j = wo1_at(final) + 3 * r + hf
                        bank = bank_for_read(act, "p1", j, b, PER1)
                        has_read(af(O1T[r % 2][:, hf * 4:hf * 4 + 4, :], bank[:].rearrange("p (k q) -> p k q", k=4),
                                    ACT.Copy), "p1", j)

            attention1(0)
            with act.Fori(1, B - 1) as b:
                attention1(b)
            attention1(B - 1, final=True)
            ln_part(4, "ln4", split=True)
            act.wait_ge(s_rt["in1"], 1)
            af(lg2[:, :, 0:E1], lg2[:, :, 0:E1], ACT.Exp).then_inc(s_rt["exp1"], 1)

        @block.vector
        def _(dve):
            v = nc.vector
            done = [0]

            def link(ins):
                done[0] += 1
                ins.then_inc(chain, 1)
                dve.wait_ge(chain, done[0])

            def ln_part(t, name, src, dst, ready=None, first=0):
                for tb in range(first, TB):
                    if ready:
                        ready(tb)
                    last = v.bn_stats(st[:, tb, :], src(tb))
                link(last)
                for tb in range(TB):
                    last = v.bn_aggr(mv[:, tb, :], st[:, tb, :])
                last.then_inc(ln_sem[t]["var"], 1)
                dve.wait_ge(ln_sem[t]["sd"], 1)
                link(v.reciprocal(rstd[:], sd[:]))
                for tb in range(TB):
                    if name and tb >= 4:
                        i, k = slot(name, tb - 4)
                        dve.wait_ge(g_full[i], k + 1)
                    v.tensor_scalar(dst(tb), src(tb), mv[:, tb, 0:1], rstd[:, tb:tb + 1], ALU.subtract, ALU.mult)\
                        .then_inc(ln_sem[t]["nrm"], 1)

            def values(name, row):
                for tb in range(TB):
                    bank = bank_for_read(dve, name, 8 + tb)
                    has_read(v.tensor_tensor(VE[:, tb, :, 0:DH0], bank[:, 0:D].rearrange("p (h d) -> p h d", d=DH0),
                                             rows0[:, row].rearrange("p (h d) -> p h d", d=DH0), ALU.add),
                             name, 8 + tb)

            def spread(out, bank, bcol, mask):
                n, m = out.shape[1], out.shape[2]
                return v.scalar_tensor_tensor(out, bank.unsqueeze(2).to_broadcast([P, n, m]),
                                              cols[:, bcol:bcol + 1], mask[:].unsqueeze(1).to_broadcast([P, n, m]),
                                              ALU.add, ALU.mult)

            def spread0(name, bcol, hh, b, part, parts):
                per, j = HH * (1 + HG if name == "q0" else 1), hh * (1 + HG if name == "q0" else 1)
                bank = bank_for_read(dve, name, j, b, per)
                if name == "q0":
                    dve.wait_ge(s_qhi, b * HH + hh + 1)
                n = S // parts
                ins = spread(QB[:, hh, part * n:part * n + n], bank[:, part * n:part * n + n], bcol + hh, hm4)
                if name == "qf" and part == parts - 1:
                    has_read(ins, name, j)

            def low_parts(hh, b):
                per, j = HH * (1 + HG), hh * (1 + HG)
                bank = bank_for_read(dve, "q0", j, b, per)
                bq = COLS["bq0"] + hh
                has_read(v.scalar_tensor_tensor(qlo[:], bank[:], cols[:, bq:bq + 1], qhi[:].bitcast(F32),
                                                ALU.add, ALU.subtract), "q0", j)

            def spread_repeated(hh, b, h):
                per, j = HH * (1 + HG), hh * (1 + HG) + 1 + h
                bank = bank_for_read(dve, "q0", j, b, per)
                has_read(v.tensor_tensor(RB[:, hh, :, :, h], bank[:].rearrange("p (a g) -> p a g", g=8),
                                         hm4[:].unsqueeze(1).to_broadcast([P, S // 8, 8]), ALU.mult), "q0", j)

            def prepare0(rel, b, n, last):
                hh, n = divmod(n, NU)
                if last and hh == HH - 1:
                    return
                nb, nh = (b, 1) if hh == 0 else (b + 1, 0)
                if n in SPREAD_AT:
                    spread0("q0" if rel else "qf", COLS["bq0" if rel else "bqkv"], nh, nb, SPREAD_AT.index(n),
                            len(SPREAD_AT))
                if rel and n == QLO_AT:
                    low_parts(nh, nb)
                if rel and n in SEL_AT:
                    spread_repeated(nh, nb, SEL_AT.index(n))

            def negmax(a, b, n, per, tiles, w):
                dve.wait_ge(a.sc, b * per + n + 1)
                if n >= 4:
                    dve.wait_ge(a.ex, b * per + n - 3)
                v.tensor_reduce(nm[:, n % 4 * 4:n % 4 * 4 + tiles],
                                SC[n % 3][:, 0:tiles * w].rearrange("p (t w) -> p t w", w=w), AX.X, ALU.max,
                                negate=True).then_inc(a.nm, 1)

            def normalised(a, dst, heads, width, g, b, per):
                dve.wait_ge(a.pv, b * per + g + 1)
                if g:
                    dve.wait_ge(a.mu, b * per + g)
                o = OB[:, 0:heads * width].rearrange("p (h w) -> p h w", w=width)
                v.reciprocal(rec[:, 0:heads], o[:, :, width - 1]).then_inc(a.rc, 1)
                dve.wait_ge(a.rc, b * per + g + 1)
                v.tensor_tensor(dst.rearrange("p (h w) -> p h w", w=width - 1), o[:, :, 0:width - 1],
                                rec[:, 0:heads].unsqueeze(2).to_broadcast([P, heads, width - 1]), ALU.mult)\
                    .then_inc(a.mu, 1)

            def attention0(a, b, to_x, last):
                def output(g):
                    hh, r = GROUPS[g]
                    off = (b * RT + r) * D + hh * P
                    if to_x:
                        if g:
                            dve.wait_ge(a.o, b * NG + g)
                        normalised(a, tmp[:], HG, VW0, g, b, NG)
                        dve.wait_ge(a.mu, b * NG + g + 1)
                        x = X[:].rearrange("p t d -> p (t d)")[:, bass.ds(off, P)]
                        v.tensor_tensor(x, x, tmp[:], ALU.add).then_inc(a.o, 1)
                    else:
                        normalised(a, ON[:].rearrange("p t d -> p (t d)")[:, bass.ds(off, P)], HG, VW0, g, b, NG)

                for n in range(NUA):
                    _, r, _, tiles = ALL_UNITS[n]
                    negmax(a, b, n, NUA, tiles, P * (r + 1))
                    prepare0(to_x, b, n, last)
                    if n - 1 in PV_DONE:
                        output(PV_DONE.index(n - 1))
                for g in range(NG):
                    if PV_DONE[g] >= NUA - 1:
                        output(g)
                dve.wait_ge(a.o if to_x else a.mu, b * NG + NG)

            v.memset(VE[:, :, :, DH0:VW0], 1.0).then_inc(s_init, 1)
            v.memset(lg[:], LOW).then_inc(s_init, 1)
            dve.wait_ge(ld["const"], 16 * 9)
            v.tensor_copy(idb[:], idf[:]).then_inc(s_init, 1)
            v.tensor_copy(maskb[:], mask_f[:]).then_inc(s_init, 1)
            v.tensor_copy(sel[:], sel_f[:]).then_inc(s_init, 1)
            values("kv0", 0)
            dve.wait_ge(ld["x"], 16)
            dve.wait_ge(s_init, 5)
            ln_part(0, "ln0", lambda tb: X[:, tb], lambda tb: nrm[:, tb % 4])
            spread0("q0", COLS["bq0"], 0, 0, 0, 1)
            low_parts(0, 0)
            for h in range(HG):
                spread_repeated(0, 0, h)
            with dve.Fori(0, B - 1) as b:
                attention0(at0, b, True, False)
            attention0(at0, B - 1, True, True)

            dve.wait_ge(at0.o, NG * B)
            ln_part("h", None, lambda tb: X[:, tb], lambda tb: Hs[:, tb])
            dve.wait_ge(ln_sem["h"]["nrm"], TB)
            ln_part(1, "ln1", lambda tb: Hs[:, tb], lambda tb: nrm[:, tb % 4])
            values("kvf", 1)
            spread0("qf", COLS["bqkv"], 0, 0, 0, 1)
            with dve.Fori(0, B - 1) as b:
                attention0(atf, b, False, False)
            attention0(atf, B - 1, False, True)
            for tb in range(TB):
                bank = bank_for_read(dve, "wo", tb)
                dve.wait_ge(s_hb, tb + 1)
                has_read(v.tensor_tensor(Hs[:, tb], bank[:, 0:D], Hs[:, tb], ALU.add), "wo", tb)
            ln_part(2, None, lambda tb: Hs[:, tb], lambda tb: NM[:, tb],
                    ready=lambda tb: wait_stored(dve, "wo", tb))

            def top_mask(width, k):
                for tb in range(TB):
                    last = v.max(top[:, tb, :], lg[:, tb, 0:width + 8])
                link(last)
                link(v.memset(top[:, :, k:8], LOW))
                for tb in range(TB):
                    last = v.match_replace(lg2[:, tb, 0:width + 8], top[:, tb, :], lg[:, tb, 0:width + 8], LOW)
                link(last)
                link(v.tensor_tensor(gat[:, :, 0:width], lg2[:, :, 0:width], lg[:, :, 0:width], ALU.not_equal))

            def over(col, width):
                return col.unsqueeze(2).to_broadcast([P, TB, width])

            bank = bank_for_read(dve, "rt0", 0)
            ins = v.tensor_copy(lg[:, :, 0:E0], bank[:, 0:TB * E0].rearrange("p (t e) -> p t e", e=E0))
            has_read(ins, "rt0", 0)
            wait_stored(dve, "rt0", 0)
            v_max = top[:, :, 0]
            for tb in range(TB):
                last = v.max(top[:, tb, :], lg[:, tb, 0:E0 + 8])
            link(last)
            link(v.tensor_copy(gA[:], v_max))
            link(v.memset(msk[:], 0.0))
            top_mask(E0, TOP0)
            v.tensor_copy(msk[:, 0:TB, :], gat[:, :, 0:E0]).then_inc(s_rt["mask"], 1)
            v.tensor_tensor(lg2[:, :, 0:E0], lg[:, :, 0:E0], over(gA[:], E0), ALU.subtract).then_inc(s_rt["in0"], 1)
            dve.wait_ge(s_rt["exp0"], 1)
            link(v.tensor_tensor(gat[:, :, 0:E0], gat[:, :, 0:E0], lg2[:, :, 0:E0], ALU.mult))
            link(v.tensor_reduce(gA[:], gat[:, :, 0:E0], AX.X, ALU.add))
            link(v.reciprocal(gB[:], gA[:]))
            v.tensor_tensor(gat[:, :, 0:E0], gat[:, :, 0:E0], over(gB[:], E0), ALU.mult).then_inc(s_gate, 1)

            k128, upto = rtab[:, 0:TB], rtab[:, TB:TB + E0 * E0].rearrange("p (a b) -> p a b", b=E0)
            jtab, etab = rtab[:, TB + E0 * E0:NTAB - E0], rtab[:, NTAB - E0:]
            tiles, ends, diff, starts = small
            dve.wait_ge(ld["route"], 32)
            bank = bank_for_read(dve, "rank", 0)
            has_read(v.tensor_copy(rk[:], bank[:, 0:(TB + 1) * E0].rearrange("p (t e) -> p t e", e=E0)), "rank", 0)
            wait_stored(dve, "rank", 0)
            link(v.tensor_tensor(lg2[:, 0:E0, 0:TB], rk[:, TB, :].unsqueeze(2).to_broadcast([P, E0, TB]),
                                 k128.unsqueeze(1).to_broadcast([P, E0, TB]), ALU.is_gt))
            link(v.tensor_reduce(tiles[:], lg2[:, 0:E0, 0:TB], AX.X, ALU.add))
            link(v.tensor_tensor(lg2[:, 0:E0, 0:E0], tiles[:].unsqueeze(1).to_broadcast([P, E0, E0]), upto, ALU.mult))
            link(v.tensor_reduce(ends[:], lg2[:, 0:E0, 0:E0], AX.X, ALU.add))
            link(v.tensor_tensor(diff[:], ends[:], tiles[:], ALU.subtract))
            link(v.tensor_scalar(starts[:], diff[:], float(P), 1.0, ALU.mult, ALU.add))
            link(v.tensor_tensor(rk[:, 0:TB, :], rk[:, 0:TB, :], starts[:].unsqueeze(1).to_broadcast([P, TB, E0]),
                                 ALU.add))
            link(v.tensor_tensor(rk[:, 0:TB, :], rk[:, 0:TB, :], msk[:, 0:TB, :], ALU.mult))
            link(v.tensor_reduce(pos_f[0][:], rk[:, 0:TB, :], AX.X, ALU.max))
            link(v.tensor_reduce(gA[:], rk[:, 0:TB, :], AX.X, ALU.add))
            link(v.tensor_tensor(pos_f[1][:], gA[:], pos_f[0][:], ALU.subtract))
            for i in range(TOP0):
                v.tensor_scalar(pos[i][:], pos_f[i][:], 1.0, None, ALU.subtract).then_inc(s_e["idx"], 1)
            for i in range(TOP0):
                link(v.tensor_tensor(lg2[:, :, 0:E0], rk[:, 0:TB, :], over(pos_f[i][:], E0), ALU.is_equal))
                link(v.tensor_tensor(lg2[:, :, 0:E0], lg2[:, :, 0:E0], gat[:, :, 0:E0], ALU.mult))
                link(v.tensor_reduce(gpair[i][:], lg2[:, :, 0:E0], AX.X, ALU.add))
            each = jtab.unsqueeze(2).to_broadcast([P, NT0, E0])
            link(v.tensor_tensor(pick[:], ends[:].unsqueeze(1).to_broadcast([P, NT0, E0]), each, ALU.is_le))
            link(v.tensor_reduce(te_f[:], pick[:], AX.X, ALU.add))
            link(v.tensor_scalar(te_f[:], te_f[:], float(E0 - 1), None, ALU.min))
            v.tensor_copy(te[:], te_f[:]).then_inc(s_e["te"], 1)
            link(v.tensor_tensor(pick[:], te_f[:].unsqueeze(2).to_broadcast([P, NT0, E0]),
                                 etab.unsqueeze(1).to_broadcast([P, NT0, E0]), ALU.is_equal))
            dve.wait_ge(ld["late"], 80)
            for f in range(FK):
                link(v.tensor_tensor(prod[:], pick[:], B1[:, f, :].unsqueeze(1).to_broadcast([P, NT0, E0]), ALU.mult))
                link(v.tensor_reduce(B1t[:, :, f], prod[:], AX.X, ALU.add))
            for tb in range(TB):
                dve.wait_ge(s_e["y"], tb + 1)
                dve.wait_ge(s_xh, tb + 1)
                v.tensor_tensor(X[:, tb], PS[2 + tb % 4][:, 0:D], X[:, tb], ALU.add).then_inc(s_e["x"], 1)

            def outputs(j, s, stored):
                dve.wait_ge(s_e["yp"], j + 1)
                if stored is not None:
                    dve.wait_ge(s_yst[s], stored)
                v.tensor_copy(ysb[s][:], PS[5][:, 0:D]).then_inc(s_e["ys"], 1)

            def moe0_tile(j, s, stored, first=False):
                if not isinstance(j, int) or j >= 2:
                    dve.wait_ge(s_e["hT"], j - 1)
                v.tensor_scalar(b1c[s][:], B1t[:].rearrange("p j f -> p (j f)")[:, bass.ds(j * FK, FK)], 0.0, None,
                                ALU.add).then_inc(s_e["b1"], 1)
                for hf in range(2):
                    dve.wait_ge(s_e["f"], 2 * j + 1 + hf)
                    if not first and hf == 0:
                        dve.wait_ge(s_e["tr"], 2 * j)
                    v.tensor_copy(hS[:, hf * 512:hf * 512 + 512], PS[1 + hf][:]).then_inc(s_e["hS"], 1)
                if not first:
                    outputs(j - 1, 1 - s, stored)

            dve.wait_ge(s_e["x"], TB)
            moe0_tile(0, 0, None, first=True)
            moe0_tile(1, 1, None)
            moe0_tile(2, 0, None)
            moe0_tile(3, 1, 16)
            with dve.Fori(2, NT0 // 2) as jp:
                for s in range(2):
                    moe0_tile(2 * jp + s, s, 16 * jp - 16 + 16 * s)
            outputs(NT0 - 1, 1, 16 * (NT0 // 2) - 16)

            def keys_values1(b):
                name, at, turn, per = kv1_use(b)
                for m in range(HP):
                    bank = bank_for_read(dve, name, at + m, turn, per)
                    dve.wait_ge(s_khi, b * HP + m + 1)
                    has_read(v.scalar_tensor_tensor(K1lo[:, m, :], bank[:], cols[:, COLS["bk1"] + m:COLS["bk1"] + m + 1],
                                                    K1hi[:].bitcast(F32)[:, m, :], ALU.add, ALU.subtract),
                             name, at + m)
                for r in range(RT):
                    for hf in range(2):
                        j = at + HP + 2 * r + hf
                        bank = bank_for_read(dve, name, j, turn, per)
                        has_read(v.tensor_tensor(V1[:, r, hf * 8:hf * 8 + 8, 0:DH1],
                                                 bank[:].rearrange("p (h d) -> p h d", d=DH1),
                                                 rows1[:, hf * S:hf * S + S].rearrange("p (h d) -> p h d", d=DH1),
                                                 ALU.add), name, j)

            link(v.memset(V1[:, :, :, DH1:VW1], 1.0))
            dve.wait_ge(ld["rows1"], 32)
            keys_values1(0)
            def combine(tb):
                dve.wait_ge(s_yp[tb // 4], 8 * 16)
                for i in range(TOP0):
                    link(v.scalar_tensor_tensor(X[:, tb], YP[i][:, tb, :], gpair[i][:, tb:tb + 1], X[:, tb],
                                                ALU.mult, ALU.add))

            ln_part(3, "ln3", lambda tb: X[:, tb], lambda tb: nrm[:, tb % 4], ready=combine)

            def attention1(b, final=False):
                def queries(p, step):
                    bank = bank_for_read(dve, "p1", p, b, PER1)
                    bias = cols[:, COLS["bq1"] + p:COLS["bq1"] + p + 1]
                    if step == 0:
                        if p:
                            wait_stored(dve, "p1", p - 1, b, PER1)
                        v.tensor_scalar(q1hi[:], bank[:], bias, None, ALU.add).then_inc(s_q1, 1)
                        return
                    dve.wait_ge(s_q1, b * (2 * HP) + 2 * p + (1 if step == 1 else 2))
                    if step == 1:
                        v.scalar_tensor_tensor(q1lo[:], bank[:], bias, q1hi[:].bitcast(F32), ALU.add, ALU.subtract)\
                            .then_inc(s_q1, 1)
                        return
                    part, out = (q1hi, QBhi[p % 2]) if step < 4 else (q1lo, QBlo[p % 2])
                    n = S // 2
                    at = step % 2 * n
                    ins = v.tensor_tensor(out[:, at:at + n, :],
                                          part[:].bitcast(F32)[:, at:at + n].unsqueeze(2).to_broadcast([P, n, 2]),
                                          hm8[:].unsqueeze(1).to_broadcast([P, n, 2]), ALU.mult)
                    if step == 5:
                        has_read(ins, "p1", p)

                def output(g):
                    p, r = divmod(g, 4)
                    normalised(at1, O1[:, r, p * P:p * P + P], 2, VW1, g, b, 32)

                for step in range(6):
                    queries(0, step)
                for n in range(64):
                    negmax(at1, b, n, 64, 1, S)
                    if 1 <= n % 8 < 7 and n < 56:
                        queries(n // 8 + 1, n % 8 - 1)
                    if n >= 6 and n % 2 == 0:
                        output((n - 6) // 2)
                for g in range(29, 32):
                    output(g)
                dve.wait_ge(at1.mu, b * 32 + 32)
                if not final:
                    keys_values1(b + 1)
                else:
                    wait_stored(dve, "p1", wo1_at(False) + 3 * RT - 1, B - 2, PER1)
                    for tb in range(TB - RT):
                        v.bn_stats(st[:, tb, :], X[:, tb])
                for r in range(RT):
                    bank = bank_for_read(dve, "p1", wo1_at(final) + 3 * r + 2, b, PER1)
                    dve.wait_ge(s_xb, TB)
                    x = X[:].rearrange("p t d -> p (t d)")[:, bass.ds((b * RT + r) * D, D)]
                    has_read(v.tensor_tensor(x, bank[:, 0:D], x, ALU.add), "p1", wo1_at(final) + 3 * r + 2)

            attention1(0)
            with dve.Fori(1, B - 1) as b:
                attention1(b)
            attention1(B - 1, final=True)
            wait_all_stored(dve, "p1")
            ln_part(4, "ln4", lambda tb: X[:, tb], lambda tb: nrm[:, tb % 4], first=TB - RT)

            def split_weights(pair, i):
                w = WE[:, :, bass.ds(2 * pair, 2), :].rearrange("p k e n -> p k (e n)")
                v.tensor_scalar(WEhi[i][:], w, 1.0, None, ALU.mult).then_inc(s_wh, 1)
                dve.wait_ge(s_wh, pair + 1)
                v.scalar_tensor_tensor(WElo[i][:], w, 1.0, WEhi[i][:].bitcast(F32), ALU.mult, ALU.subtract)\
                    .then_inc(s_ws, 1)

            dve.wait_ge(ld["we0"], 16 * DK)
            split_weights(0, 0)

            bank = bank_for_read(dve, "rt1", 0)
            has_read(v.tensor_tensor(lg[:, :, 0:E1], bank[:, 0:TB * E1].rearrange("p (t e) -> p t e", e=E1),
                                     rb_row[:].unsqueeze(1).to_broadcast([P, TB, E1]), ALU.add), "rt1", 0)
            wait_stored(dve, "rt1", 0)
            link(v.tensor_reduce(gA[:], lg[:, :, 0:E1], AX.X, ALU.max))
            v.tensor_tensor(lg2[:, :, 0:E1], lg[:, :, 0:E1], over(gA[:], E1), ALU.subtract).then_inc(s_rt["in1"], 1)
            dve.wait_ge(s_rt["exp1"], 1)
            link(v.tensor_reduce(gA[:], lg2[:, :, 0:E1], AX.X, ALU.add))
            link(v.reciprocal(gB[:], gA[:]))
            link(v.tensor_tensor(lg[:, :, 0:E1], lg2[:, :, 0:E1], over(gB[:], E1), ALU.mult))
            top_mask(E1, TOP1)
            link(v.tensor_tensor(gat[:], gat[:], lg[:, :, 0:E1], ALU.mult))
            link(v.tensor_reduce(gA[:], gat[:], AX.X, ALU.add))
            link(v.tensor_scalar(gA[:], gA[:], EPS, None, ALU.add))
            link(v.reciprocal(gB[:], gA[:]))
            link(v.tensor_tensor(gat[:], gat[:], over(gB[:], E1), ALU.mult))
            link(v.tensor_reduce(gC[:], gat[:], AX.X, ALU.add))
            link(v.tensor_scalar(gA[:], gC[:], EPS, None, ALU.max))
            link(v.reciprocal(gB[:], gA[:]))
            link(v.tensor_tensor(gat[:], gat[:], over(gB[:], E1), ALU.mult))
            link(v.tensor_scalar(gC[:], gC[:], EPS, None, ALU.mult))
            for tb in range(TB):
                v.tensor_scalar(X[:, tb], X[:, tb], gC[:, tb:tb + 1], None, ALU.add).then_inc(s_m1, 2)
            gat_flat = gat[:].rearrange("p t e -> p (t e)")

            def turn(eq, i, last=False):
                for tb, o in SUMS:
                    if o == 0:
                        dve.wait_ge(s_y1, eq * (2 * TB) + i * TB + tb + 1)
                        dve.wait_ge(s_m1, eq * (4 * TB) + (i + 1) * (2 * TB))
                    else:
                        dve.wait_ge(s_m1, eq * (4 * TB) + (i + 1) * (2 * TB) + SUMS.index((tb, 0)) + 1)
                    v.scalar_tensor_tensor(X[:, tb], PS[tb % 8][:, o * D:o * D + D],
                                           gat_flat[:, bass.ds(4 * eq + 2 * i + tb * E1 + o, 1)], X[:, tb],
                                           ALU.mult, ALU.add).then_inc(s_m1, 1)
                    if (tb, o) == (2, 0) and not last:
                        split_weights(eq * 2 + i + 1, 1 - i)

            dve.wait_ge(ld["we"], 16 * DK)
            with dve.Fori(0, E1 // 4 - 1) as eq:
                for i in range(2):
                    turn(eq, i)
            turn(E1 // 4 - 1, 0)
            turn(E1 // 4 - 1, 1, last=True)


def kernel(**inputs):
    import numpy as np
    import concourse.bacc as bacc
    from concourse.bass_utils import run_bass_kernel_spmd

    x = {k: np.asarray(a) for k, a in inputs.items()}
    f = np.float32
    col = lambda a, n: a.reshape(n, P).T
    packed = np.concatenate([
        col(x["L0_xattn_bq"], 2), col(x["L0_xattn_bk"], 2), col(x["L0_ffn_ln1_w"], 2), col(x["L0_ffn_ln1_b"], 2),
        col(x["L0_ffn_ln2_w"], 2), col(x["L0_ffn_ln2_b"], 2), col(x["L0_ffn_bqkv"], 6),
        col(x["L1_xattn_bq"], HP), col(x["L1_xattn_bk"], HP)], axis=1)
    p = np.arange(P)
    masks = np.zeros((P, 8, P), f)
    for s in range(8):
        masks[:, s] = np.where(p[None, :] > IT * s + (p // HG)[:, None], f(-1e30), f(0))
    selm = np.zeros((P, HG, P), f)
    for h in range(HG):
        selm[:, h] = (p[:, None] // DH0 == h) & (p[:, None] % DH0 == p[None, :] % DH0)
    arrays = {
        "x": x["x"].reshape(T, D), "ctxT": x["ctx_1024"].reshape(T, D).T,
        "wq0T": x["L0_xattn_Wq"].T, "wk0T": x["L0_xattn_Wk"].T, "wv0T": x["L0_xattn_Wv"].T,
        "ErT": x["L0_xattn_Er"].T, "bv0": x["L0_xattn_bv"], "bvf": x["L0_ffn_bqkv"][2 * D:], "bof": x["L0_ffn_bo"],
        "cols": packed, "ident": np.eye(P, dtype=f),
        "hm4": np.where(p[:, None] // DH0 == np.arange(HG)[None, :], f(DH0 ** -0.5), f(0)),
        "hm8": np.where(p[:, None] // DH1 == np.arange(2)[None, :], f(DH1 ** -0.5), f(0)),
        "sel": selm, "maskc": masks,
        "wqkv": x["L0_ffn_Wqkv"], "wo": x["L0_ffn_Wo"], "gate_w": x["L0_ffn_gate_W"],
        "fc1T": x["L0_ffn_fc1_w"].transpose(0, 2, 1), "fc2T": x["L0_ffn_fc2_w"].transpose(0, 2, 1),
        "fc1b": x["L0_ffn_fc1_b"].reshape(E0, FK, P).transpose(2, 1, 0),
        "rconst": np.concatenate([p[:, None] < p[None, :], np.ones((P, P), bool)], axis=1).astype(f),
        "rtab": np.tile(np.concatenate([P * np.arange(TB), np.tri(E0).reshape(-1), np.arange(NT0), np.arange(E0)])
                        .astype(f), (P, 1)), "fc2b": x["L0_ffn_fc2_b"],
        "wq1": x["L1_xattn_Wq"].reshape(D, H1 * DH1), "wk1": x["L1_xattn_Wk"].reshape(D, H1 * DH1),
        "wv1": x["L1_xattn_Wv"].reshape(D, H1 * DH1), "wo1": x["L1_xattn_Wo"].reshape(H1 * DH1, D),
        "bv1": x["L1_xattn_bv"].reshape(-1), "bo1": x["L1_xattn_bo"],
        "rwT": x["L1_ffn_router_w"].T, "rb": x["L1_ffn_router_b"], "we": x["L1_ffn_expert_w"],
    }
    nc = bacc.Bacc("TRN2", target_bir_lowering=False, num_devices=1)
    given, A = {}, {}
    for name, a in arrays.items():
        a = np.ascontiguousarray(a)
        given[f"in_{name}"] = a
        A[name] = nc.dram_tensor(f"in_{name}", a.shape, mybir.dt.from_np(a.dtype), kind="ExternalInput").ap()
    out = nc.dram_tensor("out_0", (T, D), F32, kind="ExternalOutput").ap()
    build(nc, A, out)
    r = run_bass_kernel_spmd(nc, [given], core_ids=[0])
    return r.results[0]["out_0"].reshape(B, S, D)
```
